# Optimizing a Trainium2 kernel written in Bass

```python
import numpy as np
import jax
import jax.numpy as jnp

def _softmax(x, axis=-1):
    return jax.nn.softmax(x, axis=axis)

def _gelu(x):
    return jax.nn.gelu(x, approximate=True)

def _silu(x):
    return jax.nn.silu(x)

def _sigmoid(x):
    return jax.nn.sigmoid(x)

def _layernorm(x, axis=-1, eps=1e-05):
    m = jnp.mean(x, axis=axis, keepdims=True)
    v = jnp.var(x, axis=axis, keepdims=True)
    return (x - m) / jnp.sqrt(v + eps)

def _scatter_add(tgt, idx, src, axis=0):
    return tgt.at[idx].add(src)

def _segment_sum(src, seg, n):
    return jax.ops.segment_sum(src, seg, n)
kernel_name = 'mk_macaron_d1_jaxref_r4_e17090'

def setup_inputs(seed: int=0):
    np.random.seed(seed)
    _w = jnp.asarray

    def _L0_attn_setup():
        import jax, jax.numpy as jnp
        import numpy as np
        H = 16

        def _alibi_slopes(n):
            start = 2.0 ** (-2.0 ** (-(np.log2(n) - 3)))
            return np.array([start * start ** i for i in range(n)], dtype=np.float32)
        key = jax.random.key(seed)
        ks = jax.random.split(key, 6)
        B, L, C = (2, 512, 256)
        scale = 0.02
        return {'q': jax.random.normal(ks[0], (B, L, C), dtype=jnp.float32), 'Wq': jax.random.normal(ks[1], (C, C), dtype=jnp.float32) * scale, 'Wk': jax.random.normal(ks[2], (C, C), dtype=jnp.float32) * scale, 'Wv': jax.random.normal(ks[3], (C, C), dtype=jnp.float32) * scale, 'Wo': jax.random.normal(ks[4], (C, C), dtype=jnp.float32) * scale, 'bo': jax.random.normal(ks[5], (C,), dtype=jnp.float32) * scale}
    _L0_attn_in = _L0_attn_setup()

    def _L0_ffn_setup():
        import jax, jax.numpy as jnp
        import numpy as np
        DIM = 256
        HIDDEN = 768
        SCALE = 1.0 / 127.0

        def _dequant(w_int, dtype):
            return w_int.astype(dtype) * jnp.asarray(SCALE, dtype)
        key = jax.random.key(seed)
        k_x, k_g, k_u, k_d = jax.random.split(key, 4)
        x = jax.random.normal(k_x, (4, 512, DIM), dtype=jnp.float32)
        w_gate = jax.random.randint(k_g, (HIDDEN, DIM), -127, 128, dtype=jnp.int32)
        w_up = jax.random.randint(k_u, (HIDDEN, DIM), -127, 128, dtype=jnp.int32)
        w_down = jax.random.randint(k_d, (DIM, HIDDEN), -127, 128, dtype=jnp.int32)
        return {'x': x, 'w_gate': w_gate, 'w_up': w_up, 'w_down': w_down}
    _L0_ffn_in = _L0_ffn_setup()
    _d = {'L0_attn_q': _L0_attn_in['q'], 'L0_attn_Wq': _L0_attn_in['Wq'], 'L0_attn_Wk': _L0_attn_in['Wk'], 'L0_attn_Wv': _L0_attn_in['Wv'], 'L0_attn_Wo': _L0_attn_in['Wo'], 'L0_attn_bo': _L0_attn_in['bo'], 'L0_ffn_w_gate': _L0_ffn_in['w_gate'], 'L0_ffn_w_up': _L0_ffn_in['w_up'], 'L0_ffn_w_down': _L0_ffn_in['w_down']}
    _x0 = _d['L0_attn_q']
    _d['L0_attn_q'] = jax.random.normal(jax.random.fold_in(jax.random.key(seed), 1), (8, 512, 256), dtype=_x0.dtype)
    del _x0
    return _d

def reference(L0_attn_q, L0_attn_Wq, L0_attn_Wk, L0_attn_Wv, L0_attn_Wo, L0_attn_bo, L0_ffn_w_gate, L0_ffn_w_up, L0_ffn_w_down):

    def _L0_attn_ref(q, Wq, Wk, Wv, Wo, bo):
        import jax, jax.numpy as jnp
        import numpy as np
        H = 16

        def _alibi_slopes(n):
            start = 2.0 ** (-2.0 ** (-(np.log2(n) - 3)))
            return np.array([start * start ** i for i in range(n)], dtype=np.float32)
        B, L, C = q.shape
        D = C // H
        inv_sqrt_d = jnp.asarray(D, q.dtype) ** (-0.5)

        def proj(x, W):
            return (x @ W.T).reshape(B, L, H, D).transpose(0, 2, 1, 3)
        qh, kh, vh = (proj(q, Wq), proj(q, Wk), proj(q, Wv))
        pos = jnp.arange(L)
        rel = jnp.abs(pos[None, :] - pos[:, None]).astype(q.dtype)
        slopes = jnp.asarray(_alibi_slopes(H), dtype=q.dtype)
        bias = (-slopes)[:, None, None] * rel
        scores = jnp.einsum('bhld,bhsd->bhls', qh, kh) * inv_sqrt_d + bias[None]
        attn = jax.nn.softmax(scores, axis=-1)
        out = jnp.einsum('bhls,bhsd->bhld', attn, vh)
        out = out.transpose(0, 2, 1, 3).reshape(B, L, C)
        return out @ Wo.T + bo

    def _L0_ffn_ref(x, w_gate, w_up, w_down):
        import jax, jax.numpy as jnp
        import numpy as np
        DIM = 256
        HIDDEN = 768
        SCALE = 1.0 / 127.0

        def _dequant(w_int, dtype):
            return w_int.astype(dtype) * jnp.asarray(SCALE, dtype)
        wg = _dequant(w_gate, x.dtype)
        wu = _dequant(w_up, x.dtype)
        wd = _dequant(w_down, x.dtype)
        gate = jnp.einsum('bsd,hd->bsh', x, wg)
        up = jnp.einsum('bsd,hd->bsh', x, wu)
        h = jax.nn.silu(gate) * up
        return jnp.einsum('bsh,dh->bsd', h, wd)
    x = L0_attn_q
    x = x + 0.5 * _L0_ffn_ref(_layernorm(x, axis=-1), L0_ffn_w_gate, L0_ffn_w_up, L0_ffn_w_down)
    x = x + _L0_attn_ref(_layernorm(x, axis=-1), L0_attn_Wq, L0_attn_Wk, L0_attn_Wv, L0_attn_Wo, L0_attn_bo)
    x = x + 0.5 * _L0_ffn_ref(_layernorm(x, axis=-1), L0_ffn_w_gate, L0_ffn_w_up, L0_ffn_w_down)
    return x

_drawn_inputs = setup_inputs


def setup_inputs(seed=0):
    import zlib

    import numpy as np

    out = dict(_drawn_inputs(seed))
    spreads = {}
    factors = {'L0_attn_Wq': 35.652,
     'L0_attn_Wk': 35.332,
     'L0_attn_Wv': 34.73,
     'L0_attn_Wo': 34.803,
     'L0_attn_bo': 64.0}
    for name, (base, spread) in spreads.items():
        noise = np.random.default_rng([zlib.crc32(name.encode()), seed]).standard_normal(out[name].shape)
        drawn = base * np.exp(spread * noise) if base else spread * noise
        out[name] = jnp.asarray(drawn.astype(out[name].dtype))
    for name, factor in factors.items():
        out[name] = (out[name] * factor).astype(out[name].dtype)
    return out
```

```python
from contextlib import ExitStack

import numpy as np

import concourse.bass as bass
from concourse import mybir

F32 = mybir.dt.float32
F32R = mybir.dt.float32r
I32 = mybir.dt.int32
ALU = mybir.AluOpType
ACT = mybir.ActivationFunctionType

P = 128
B, L, C = 8, 512, 256
H, D = 16, 16
FF = 768
TT = L // P
KC = C // P
FT = FF // P
QH = 4
NQ = H // QH
STEPS = 2 * TT
LEAD = 12
SEG = 64
NSEG = L // SEG
ROW_BIAS = 4 * D
ROW_MAX = ROW_BIAS + 4 * NSEG
ROWS = ROW_MAX + 2
DEQ = float(np.float32(1.0 / 127.0))
EPS = 1e-5
MAGIC = float(0x5F3759DF)
NEWTON = 3
LN_OPS = 4 + 4 + 3 + 3 * NEWTON


def slopes():
    start = 2.0 ** (-2.0 ** (-(np.log2(H) - 3)))
    return np.array([start * start ** i for i in range(H)], dtype=np.float32)


def hi_lo(a):
    a = np.asarray(a, np.float32)
    u = a.view(np.uint32)
    hi = ((u + 0x7FF + ((u >> 12) & 1)) & np.uint32(0xFFFFF000)).view(np.float32)
    return hi, a - hi


def tables():
    s = slopes()
    pos = np.arange(L, dtype=np.float64)
    centre = SEG * np.arange(NSEG) + (SEG - 1) / 2
    inside = (np.arange(L)[None, :] // SEG) == np.arange(NSEG)[:, None]
    one = inside.astype(np.float32)
    off = np.where(inside, pos[None, :] - centre[:, None], 0.0).astype(np.float32)
    qb = np.zeros((4 * NSEG, H, L), np.float32)
    for h in range(H):
        a_hi, a_lo = hi_lo(one * s[h])
        b_hi, b_lo = hi_lo(off * s[h])
        qb[:, h] = np.concatenate([a_hi, a_lo, b_hi, b_lo])
    dist = (-np.abs(pos[None, :] - centre[:, None])).astype(np.float32)
    sign = np.sign(pos[None, :] - centre[:, None]).astype(np.float32)
    kb = np.concatenate([dist, dist, sign, sign, np.ones((2, L), np.float32)])
    j, i = np.arange(P)[:, None], np.arange(P)[None, :]
    t = SEG * (i // SEG) + (SEG - 1) / 2
    over = (i // SEG == j // SEG) & ((i > t) == (j > t)) & (np.abs(i - t) > np.abs(j - t))
    excess = np.where(over, 2.0 * np.abs(i - j), 0.0)
    diag = np.exp(-s.astype(np.float64)[None, :, None] * excess[:, None, :]).astype(np.float32)
    return {"q_bias": qb, "k_bias": kb, "diag_table": diag, "eye_table": np.eye(P, dtype=np.float32)}


FILLS = {
    (0, 3): "heads3_prev", (0, 4): "xt0_next", (0, 5): "max1", (0, 6): "xt1_next", (0, 7): "qk0_next",
    (1, 0): "qk1_next", (1, 2): "qk2_next", (1, 3): "heads0", (1, 4): "qk3_next", (1, 5): "max2",
    (1, 6): "v0_next", (1, 7): "turn1_prev",
    (2, 0): "v1_next", (2, 1): "out0_prev", (2, 2): "out1_prev", (2, 3): "heads1", (2, 5): "max3",
    (2, 6): "turn0",
    (3, 3): "heads2", (3, 5): "max0_next",
}
ALL_FILLS = list(FILLS.values())
FILLS_BEFORE = ["qk0_next", "qk1_next", "qk2_next", "qk3_next", "v0_next", "v1_next", "max0_next"]
FIRST_FILLS = [f for f in ALL_FILLS if not f.endswith("_prev")]
LAST_FILLS = [f for f in ALL_FILLS if not f.endswith("_next") or f.startswith("xt")]
TAIL_FILLS = ["heads3_prev", "turn1_prev", "out0_prev", "out1_prev"]


def fill_no(b, name):
    if isinstance(b, int):
        if b < 0:
            return FILLS_BEFORE.index(name)
        if b == 0:
            return len(FILLS_BEFORE) + FIRST_FILLS.index(name)
        if b >= B - 1:
            until = len(FILLS_BEFORE) + len(FIRST_FILLS) + (B - 2) * len(ALL_FILLS)
            if b == B - 1:
                return until + LAST_FILLS.index(name)
            return until + len(LAST_FILLS) + TAIL_FILLS.index(name)
    return b * len(ALL_FILLS) + (
        len(FILLS_BEFORE) + len(FIRST_FILLS) - len(ALL_FILLS) + ALL_FILLS.index(name))


def build_program(nc, d_x, d_wgu, d_wdn, d_wqkv, d_wo, d_bo, d_qb, d_kb, d_diag, d_eye, d_out):
    with ExitStack() as ctx:
        def sb(name, shape, dt=F32):
            return ctx.enter_context(nc.sbuf_tensor(name, shape, dt))

        def sem(name):
            return ctx.enter_context(nc.semaphore(name))

        x_sb = sb("x_sb", [P, B * TT * C])
        wgu = sb("wgu", [P, KC, 2 * FF])
        wdn = sb("wdn", [P, FT, C])
        wqkv = sb("wqkv", [P, KC, 3 * C])
        wo = sb("wo", [P, KC, C])
        bo = sb("bo", [P, C])
        eye = sb("eye", [P, P])
        diag = sb("diag", [P, H, P])
        q_aug = sb("q_aug", [P, H, L], F32R)
        k_aug = sb("k_aug", [P, H, L], F32R)
        v_aug = sb("v_aug", [P, TT, H, 2 * D])
        probs = sb("probs", [P, 2, QH, L])
        parts = sb("parts", [P, 2, 2, 2, L], F32R)
        xn = sb("xn", [P, TT, C])
        xnt = sb("xnt", [P, KC, L])
        v_new = sb("v_new", [P, TT, C])
        heads_t = sb("heads_t", [P, L])
        heads = sb("heads", [P, TT, C])
        att_t = sb("att_t", [P, KC, L])
        max_row = sb("max_row", [2 * QH, L], F32R)
        row_max = sb("row_max", [P, 2, TT, QH])
        max_in = sb("max_in", [P, TT, 2 * QH])
        den = sb("den", [P, TT, QH, 1])
        stats = sb("stats", [P, TT, 6])
        mean_var = sb("mean_var", [P, TT, 2])
        var = sb("var", [P, TT])
        rstd = sb("rstd", [P, TT])
        newton = sb("newton", [P, TT])
        flat = probs[:, :, :, :].rearrange("p a h q -> p (a h q)")
        hid = flat[:, 0:FT * L].rearrange("p (f q) -> p f q", f=FT)
        gated = flat[:, FT * L:(FT + 2) * L].rearrange("p (s q) -> p s q", s=2)

        ps = ctx.enter_context(nc.psum_tensor("ps", [P, 8, L], F32))
        scores_at, max_at, pv, misc = 0, 4, ps[:, 6, :], ps[:, 7, :]
        gate_at, up_at, turn_at, y_at = 0, 2, 4, 6
        misc_tiles = misc.rearrange("p (t c) -> p t c", t=2)

        x_in = [sem(f"x_loaded{b}") for b in range(B)]
        gu_in, dn_in, att_in, aug_in, stored = (sem(n) for n in ("gu_in", "dn_in", "att_in", "aug_in", "stored"))
        ln_step, xn_ready = sem("ln_step"), sem("xn_ready")
        ffn = [{n: sem(f"{n}_{w}") for n in ("turned", "xnt_ready", "gate_done", "up_done", "gated_ready",
                                             "hid_ready", "y_done", "y_used")} for w in ("a", "c")]
        ones_set, bo_added = sem("ones_set"), sem("bo_added")
        filled, drained, hi_ready = sem("filled"), sem("drained"), sem("hi_ready")
        s1_done, s1_used = sem("s1_done"), sem("s1_used")
        neg_hi, neg_ready = sem("neg_hi"), sem("neg_ready")
        aug_done = [sem(f"aug_done{n}") for n in range(NQ)]
        max_moved = sem("max_moved")
        st_done, exp_done, fixed = sem("st_done"), sem("exp_done"), sem("fixed")
        pv_done, heads_t_ready, den_ready, v_ready = (sem(n) for n in ("pv_done", "heads_t_ready", "den_ready", "v_ready"))
        block = ctx.enter_context(nc.Block())

        def wait(eng, s, value):
            if not (isinstance(value, int) and value <= 0):
                eng.wait_ge(s, value)

        def turns(eng, body):
            body(0)
            with eng.Fori(1, B - 1) as b:
                body(b)
            body(B - 1)

        def first(b):
            return isinstance(b, int) and b == 0

        def last(b):
            return isinstance(b, int) and b == B - 1

        def fills_of(b):
            return FIRST_FILLS if first(b) else LAST_FILLS if last(b) else ALL_FILLS

        def x_of(b, tile, n=1):
            at = b * (TT * C) + tile * C
            return x_sb[:, bass.ds(at, n * C)]

        def fill_parts(b, name):
            base = name.split("_")[0]
            seq = b + 1 if name.endswith("_next") else b - 1 if name.endswith("_prev") else b
            return seq, base[:-1], int(base[-1])

        @block.sync
        def _(sp):
            for b in range(B):
                sp.dma_start(x_sb[:, b * TT * C:(b + 1) * TT * C], d_x[b]).then_inc(x_in[b], 16)
                if b == 0:
                    sp.dma_start(eye[:], d_eye).then_inc(att_in, 16)
                if b == 1:
                    sp.dma_start(wqkv[:], d_wqkv.rearrange("(k p) n -> p k n", p=P)).then_inc(att_in, 16)
                    sp.dma_start(wo[:], d_wo.rearrange("(k p) n -> p k n", p=P)).then_inc(att_in, 16)
                    sp.dma_start(bo[:], d_bo.to_broadcast([P, C])).then_inc(att_in, 16)
            sp.dma_start(diag[:], d_diag).then_inc(att_in, 16)

            def spread(b, quad, made):
                if first(b):
                    sp.wait_ge(drained, made + 1)
                else:
                    steps = STEPS + 4 if quad == 0 else (quad + 1) * STEPS
                    sp.wait_ge(st_done, (b - 1) * (NQ * STEPS) + steps)
                for g in range(QH):
                    h = quad * QH + g
                    p0 = (h % 8) * D
                    for rep in range(2):
                        for part in range(2):
                            r = (2 * rep + part) * D
                            sp.dma_start(q_aug[r:r + D, h, :].bitcast(F32),
                                         parts[p0:p0 + D, h // 8, 0, part, :].bitcast(F32)).then_inc(aug_done[quad], 16)
                            r = (2 * part + rep) * D
                            sp.dma_start(k_aug[r:r + D, h, :].bitcast(F32),
                                         parts[p0:p0 + D, h // 8, 1, part, :].bitcast(F32)).then_inc(aug_done[quad], 16)

            def move_max(quad, made):
                sp.wait_ge(drained, made + 1)
                for part in range(2):
                    for g in range(QH):
                        sp.dma_start(q_aug[ROW_MAX + part:ROW_MAX + part + 1, quad * QH + g, :].bitcast(F32),
                                     max_row[part * QH + g:part * QH + g + 1, :].bitcast(F32)).then_inc(max_moved, 16)

            for quad in range(NQ):
                spread(0, quad, fill_no(-1, "qk1_next" if quad < 2 else "qk3_next"))
            move_max(0, fill_no(-1, "max0_next"))

            def turn(b):
                for n in range(NQ):
                    if n + 1 < NQ:
                        move_max(n + 1, fill_no(b, f"max{n + 1}"))
                    elif not last(b):
                        move_max(0, fill_no(b, "max0_next"))
                    if not last(b):
                        spread(b + 1, n, None)

            turns(sp, turn)

            def store(b):
                sp.wait_ge(ffn[1]["y_used"], 2 * b + 2)
                sp.dma_start(d_out[b], x_of(b, 0, TT)).then_inc(stored, 16)
            for b in range(B):
                store(b)
            sp.wait_ge(stored, 16 * B)

        @block.gpsimd
        def _(pool):
            pool.dma_start(wgu[:], d_wgu.rearrange("(k p) n -> p k n", p=P)).then_inc(gu_in, 16)
            pool.dma_start(wdn[:], d_wdn.rearrange("(k p) n -> p k n", p=P)).then_inc(dn_in, 16)
            for h in range(H):
                pool.dma_start(q_aug[ROW_BIAS:ROW_MAX, h, :], d_qb[:, h, :]).then_inc(aug_in, 16)
                pool.dma_start(k_aug[ROW_BIAS:ROWS, h, :], d_kb).then_inc(aug_in, 16)
            nc.gpsimd.memset(v_aug[:], 1.0).then_inc(ones_set, 1)
            pool.wait_ge(ones_set, 1)

            def place_v(b, quad):
                nc.gpsimd.tensor_copy(
                    v_aug[:, :, quad * QH:(quad + 1) * QH, 0:D],
                    v_new[:, :, quad * QH * D:(quad + 1) * QH * D].rearrange("p t (g d) -> p t g d", g=QH),
                ).then_inc(v_ready, 1)

            pool.wait_ge(drained, fill_no(-1, "v1_next") + 1)
            for quad in range(3):
                place_v(0, quad)
            pool.wait_ge(att_in, 16 * 5)

            def add_bo(b):
                pool.wait_ge(xn_ready, TT * (B + b) + TT)
                for tile in range(TT):
                    nc.gpsimd.tensor_tensor(x_of(b, tile), x_of(b, tile), bo[:], ALU.add).then_inc(bo_added, 1)

            add_bo(0)

            def turn(b):
                for n in range(NQ):
                    for s in range(STEPS):
                        kt, pair = s // 2, s % 2
                        g = b * (NQ * STEPS) + n * STEPS + s
                        if (n, s) == (0, 3) and not first(b):
                            pool.wait_ge(pv_done, b * (NQ * TT))
                        if (n, s) == (2, 4) and not last(b):
                            pool.wait_ge(pv_done, b * (NQ * TT) + 2 * TT)
                            pool.wait_ge(drained, fill_no(b, "v1_next") + 1)
                        if (n, s) == (3, 4) and not last(b):
                            pool.wait_ge(pv_done, b * (NQ * TT) + 3 * TT)
                        pool.wait_ge(exp_done, g + 1)
                        tile = probs[:, kt % 2, 2 * pair:2 * pair + 2, kt * P:(kt + 1) * P]
                        nc.gpsimd.tensor_tensor(tile, tile, diag[:, n * QH + 2 * pair:n * QH + 2 * pair + 2, :],
                                                ALU.mult).then_inc(fixed, 1)
                        if (n, s) == (0, 3):
                            place_v(b, 3)
                        if not last(b):
                            if (n, s) == (1, 0):
                                add_bo(b + 1)
                            if (n, s) == (2, 4):
                                place_v(b + 1, 0)
                                place_v(b + 1, 1)
                            if (n, s) == (3, 4):
                                place_v(b + 1, 2)

            turns(pool, turn)

        @block.scalar
        def _(act):
            def ffn_turn(w, b):
                s = ffn[w]
                for f in range(FT):
                    act.wait_ge(s["gate_done"], FT * b + f + 1)
                    wait(act, s["hid_ready"], FT * b + f - 1)
                    nc.scalar.activation(gated[:, f % 2, :], ps[:, gate_at + f % 2, :], ACT.Silu, scale=DEQ
                                         ).then_inc(s["gated_ready"], 1)
                if not (w == 1 and last(b)):
                    turned(w, b + 1)

            def turned(w, b):
                s = ffn[w]
                act.wait_ge(s["turned"], 2 * b + 1 - 2 * w)
                nc.scalar.copy(xnt[:, 0, :], ps[:, turn_at, :]).then_inc(s["xnt_ready"], 1)

            turned(0, 0)
            turns(act, lambda b: ffn_turn(0, b))

            def drain(b, name):
                at = fill_no(b, name)
                seq, kind, part = fill_parts(b, name)
                if kind in ("heads", "out"):
                    return
                act.wait_ge(filled, at + 1)
                if kind == "xt":
                    nc.scalar.copy(xnt[:, part, :], misc).then_inc(drained, 1)
                elif kind == "qk":
                    half, is_k = part // 2, part % 2
                    if not (isinstance(seq, int) and seq == 0):
                        for quad in (2 * half, 2 * half + 1):
                            act.wait_ge(aug_done[quad], seq * (16 * 8 * QH))
                    nc.scalar.activation(parts[:, half, is_k, 0, :], misc, ACT.Copy,
                                         scale=1.0 if is_k else D ** -0.5).then_inc(hi_ready, 1)
                elif kind == "v":
                    if not (isinstance(seq, int) and seq == 0):
                        act.wait_ge(v_ready, NQ * seq)
                    nc.scalar.copy(v_new[:, 2 * part:2 * part + 2, :], misc_tiles).then_inc(drained, 1)
                elif kind == "max":
                    quad_no = seq * NQ + part
                    wait(act, max_moved, quad_no * (16 * 2 * QH))
                    nc.scalar.copy(max_row[:, :], misc[0:2 * QH, :]).then_inc(drained, 1)
                elif kind == "turn":
                    nc.scalar.copy(att_t[:, part, :], misc).then_inc(drained, 1)

            for name in FILLS_BEFORE:
                drain(-1, name)

            def take_heads(quad_no):
                act.wait_ge(pv_done, (quad_no + 1) * TT)
                nc.scalar.copy(heads_t[:, :], pv).then_inc(heads_t_ready, 1)

            def turn(b):
                for n in range(NQ):
                    for s in range(STEPS):
                        kt, pair = s // 2, s % 2
                        quad_no = b * NQ + n
                        g = quad_no * STEPS + s
                        act.wait_ge(st_done, g + 1)
                        wait(act, pv_done, quad_no * TT + kt - 1)
                        at = scores_at + 2 * pair
                        nc.scalar.activation(probs[:, kt % 2, 2 * pair:2 * pair + 2, :], ps[:, at:at + 2, :],
                                             ACT.Exp).then_inc(exp_done, 1)
                        if s == 2 and not (first(b) and n == 0):
                            take_heads(quad_no - 1)
                        name = FILLS.get((n, s))
                        if name in fills_of(b):
                            drain(b, name)

            turns(act, turn)
            take_heads(B * NQ - 1)
            for name in TAIL_FILLS:
                drain(B, name)
            turns(act, lambda b: ffn_turn(1, b))

        @block.vector
        def _(dve):
            def ln_stats(no, b, tile):
                nc.vector.bn_stats(stats[:, tile, :], x_of(b, tile)).then_inc(ln_step, 1)

            def ln_finish(no, b):
                k = [no * LN_OPS + TT]

                def link(ins):
                    ins.then_inc(ln_step, 1)
                    k[0] += 1 if isinstance(k[0], int) else 0
                    k[0] = k[0] if isinstance(k[0], int) else k[0] + 1
                    dve.wait_ge(ln_step, k[0])

                for tile in range(TT):
                    ins = nc.vector.bn_aggr(mean_var[:, tile, :], stats[:, tile, :])
                    if tile < TT - 1:
                        ins.then_inc(ln_step, 1)
                        k[0] = k[0] + 1
                link(ins)
                link(nc.vector.tensor_scalar(var[:, :], mean_var[:, :, 1], EPS, None, ALU.add))
                link(nc.vector.tensor_scalar(rstd[:, :].bitcast(I32), var[:, :].bitcast(I32), 1, None,
                                             ALU.logical_shift_right))
                link(nc.vector.tensor_scalar(rstd[:, :].bitcast(I32), rstd[:, :].bitcast(I32), -1.0, MAGIC,
                                             ALU.mult, ALU.add))
                for _ in range(NEWTON):
                    link(nc.vector.scalar_tensor_tensor(newton[:, :], rstd[:, :], -0.5, rstd[:, :],
                                                        ALU.mult, ALU.mult))
                    link(nc.vector.tensor_tensor(newton[:, :], newton[:, :], var[:, :], ALU.mult))
                    link(nc.vector.scalar_tensor_tensor(rstd[:, :], newton[:, :], 1.5, rstd[:, :],
                                                        ALU.add, ALU.mult))
                for tile in range(TT):
                    nc.vector.tensor_scalar(xn[:, tile, :], x_of(b, tile), mean_var[:, tile, 0:1],
                                            rstd[:, tile:tile + 1], ALU.subtract, ALU.mult).then_inc(xn_ready, 1)

            def stats_ready(no):
                dve.wait_ge(ln_step, no * LN_OPS + TT)

            def turned(w, b):
                s = ffn[w]
                dve.wait_ge(s["turned"], 2 * b + 2 - 2 * w)
                nc.vector.tensor_copy(xnt[:, 1, :], ps[:, turn_at + 1, :]).then_inc(s["xnt_ready"], 1)

            def ffn_turn(w, b):
                s = ffn[w]
                then = (2 * w * B + b + 1, b + 1) if not last(b) else (B, 0) if w == 0 else None
                for f in range(FT):
                    dve.wait_ge(s["gated_ready"], FT * b + f + 1)
                    dve.wait_ge(s["up_done"], FT * b + f + 1)
                    if f == 0:
                        wait(dve, s["y_done"], 2 * b)
                    if then and f == 3:
                        stats_ready(then[0])
                        wait(dve, s["turned"], 2 * b + 2 - 2 * w)
                    nc.vector.scalar_tensor_tensor(hid[:, f, :], ps[:, up_at + f % 2, :], DEQ, gated[:, f % 2, :],
                                                   ALU.mult, ALU.mult).then_inc(s["hid_ready"], 1)
                    if then and f == 2:
                        if last(b):
                            dve.wait_ge(s["y_used"], 2)
                        for tile in range(TT):
                            ln_stats(*then, tile)
                    if then and f == 3:
                        ln_finish(*then)
                if not (w == 1 and last(b)):
                    turned(w, b + 1)
                for j in range(2):
                    dve.wait_ge(s["y_done"], 2 * b + j + 1)
                    nc.vector.scalar_tensor_tensor(x_of(b, 2 * j, 2), ps[:, y_at + j, :], 0.5 * DEQ, x_of(b, 2 * j, 2),
                                                   ALU.mult, ALU.add).then_inc(s["y_used"], 1)

            dve.wait_ge(x_in[0], 16)
            for tile in range(TT):
                ln_stats(0, 0, tile)
            stats_ready(0)
            ln_finish(0, 0)
            turned(0, 0)
            for b in range(1, B):
                dve.wait_ge(x_in[b], 16)
            turns(dve, lambda b: ffn_turn(0, b))
            dve.wait_ge(ffn[0]["y_used"], 2 * B)

            def row_maxima(unit):
                u = unit[1]
                for i in range(2):
                    dve.wait_ge(s1_done, unit[0] + i + 1)
                    nc.vector.reduce_max(row_max[:, unit[2], 2 * (u % 2) + i, u // 2:u // 2 + 1],
                                         ps[:, max_at + i, :], mybir.AxisListType.X).then_inc(s1_used, 1)

            def unit_at(b, local):
                return 2 * (b * (NQ * STEPS) + local), local % STEPS, (local // STEPS) % 2

            def negate(quad_no, slot):
                dve.wait_ge(s1_used, (quad_no + 1) * (2 * STEPS))
                m = row_max[:, slot, :, :]
                nc.vector.tensor_scalar(max_in[:, :, 0:QH].bitcast(F32R), m, -1.0, None, ALU.mult).then_inc(neg_hi, 1)
                dve.wait_ge(neg_hi, quad_no + 1)
                nc.vector.scalar_tensor_tensor(max_in[:, :, QH:2 * QH], m, -1.0, max_in[:, :, 0:QH],
                                               ALU.mult, ALU.subtract).then_inc(neg_ready, 1)

            def drain(b, name):
                at = fill_no(b, name)
                seq, kind, part = fill_parts(b, name)
                if kind == "qk":
                    half, is_k = part // 2, part % 2
                    dve.wait_ge(hi_ready, seq * 4 + part + 1)
                    nc.vector.scalar_tensor_tensor(parts[:, half, is_k, 1, :], misc, 1.0 if is_k else D ** -0.5,
                                                   parts[:, half, is_k, 0, :].bitcast(F32),
                                                   ALU.mult, ALU.subtract).then_inc(drained, 1)
                elif kind == "heads":
                    dve.wait_ge(filled, at + 1)
                    got = misc.rearrange("p (t g d) -> p t g d", t=TT, g=QH)
                    nc.vector.reciprocal(den[:, :, :, :], got[:, :, :, D:D + 1]).then_inc(den_ready, 1)
                    dve.wait_ge(den_ready, seq * NQ + part + 1)
                    nc.vector.tensor_tensor(
                        heads[:, :, part * QH * D:(part + 1) * QH * D].rearrange("p t (g d) -> p t g d", g=QH),
                        got[:, :, :, 0:D], den[:, :, :, :].to_broadcast([P, TT, QH, D]), ALU.mult
                    ).then_inc(drained, 1)
                elif kind == "out":
                    dve.wait_ge(filled, at + 1)
                    dve.wait_ge(bo_added, TT * (seq + 1))
                    xs = x_of(seq, 2 * part, 2)
                    nc.vector.tensor_tensor(xs, misc, xs, ALU.add).then_inc(drained, 1)

            for name in FILLS_BEFORE[:-1]:
                drain(-1, name)
            for u in range(LEAD):
                row_maxima(unit_at(0, u))
                if u == STEPS - 1:
                    negate(0, 0)

            def turn(b):
                then = (2 * B, 0) if last(b) else (B + b + 1, b + 1)
                for n in range(NQ):
                    for s in range(STEPS):
                        local = n * STEPS + s
                        if n == 0 and s < 4:
                            if last(b) and s == 0:
                                dve.wait_ge(drained, fill_no(1, "out1_prev") + 1)
                            ln_stats(*then, s)
                        if (n, s) == (0, 3):
                            stats_ready(then[0])
                        if not (last(b) and local + LEAD >= NQ * STEPS):
                            row_maxima(unit_at(b, local + LEAD))
                        if s == 4 and not (last(b) and n == NQ - 1):
                            negate(b * NQ + n + 1, (n + 1) % 2)
                        if (n, s) == (0, 3):
                            ln_finish(*then)
                        name = FILLS.get((n, s))
                        if name in fills_of(b):
                            drain(b, name)

            turns(dve, turn)
            for name in TAIL_FILLS:
                drain(B, name)
            dve.wait_ge(drained, fill_no(B, TAIL_FILLS[-1]) + 1)
            turns(dve, lambda b: ffn_turn(1, b))

        @block.tensor
        def _(pe):
            def matmul(out, lhs, rhs, start, stop, **k):
                return nc.tensor.matmul(out, lhs, rhs, start=start, stop=stop, **k)

            def turn_x(w, b):
                s = ffn[w]
                pe.wait_ge(xn_ready, TT * (2 * w * B + b + 1))
                if w == 1:
                    wait(pe, s["xnt_ready"], 2 * b - 2)
                else:
                    wait(pe, s["xnt_ready"], 2 * b)
                for k in range(KC):
                    for t in range(TT):
                        ins = nc.tensor.transpose(ps[:, turn_at + k, t * P:(t + 1) * P],
                                                  xn[:, t, k * P:(k + 1) * P], eye[:])
                    ins.then_inc(s["turned"], 1)

            def ffn_turn(w, b):
                s = ffn[w]
                if w == 0:
                    pe.wait_ge(s["xnt_ready"], 2 * b + 2)
                else:
                    wait(pe, s["xnt_ready"], 2 * b)
                for f in range(FT):
                    wait(pe, s["hid_ready"], FT * b + f - 1)
                    for which, at, done in ((0, gate_at, "gate_done"), (1, up_at, "up_done")):
                        for k in range(KC):
                            w0 = which * FF + f * P
                            ins = matmul(ps[:, at + f % 2, :], wgu[:, k, w0:w0 + P], xnt[:, k, :], k == 0, k == KC - 1)
                        ins.then_inc(s[done], 1)
                if not (w == 1 and last(b)):
                    turn_x(w, b + 1)
                wait(pe, s["y_used"], 2 * b)
                for f in range(FT):
                    pe.wait_ge(s["hid_ready"], FT * b + f + 1)
                    for t in range(TT):
                        out = ps[:, y_at + t // 2, (t % 2) * C:(t % 2 + 1) * C]
                        ins = matmul(out, hid[:, f, t * P:(t + 1) * P], wdn[:, f, :], f == 0 and t % 2 == 0,
                                     f == FT - 1, skip_group_check=True)
                        if f == FT - 1 and t % 2 == 1:
                            ins.then_inc(s["y_done"], 1)

            pe.wait_ge(att_in, 16 * 5)
            turn_x(0, 0)
            pe.wait_ge(gu_in, 16)
            pe.wait_ge(dn_in, 16)
            turns(pe, lambda b: ffn_turn(0, b))

            def fill(b, name):
                at = fill_no(b, name)
                seq, kind, part = fill_parts(b, name)
                wait(pe, drained, at)
                if kind == "xt":
                    pe.wait_ge(xn_ready, TT * (B + seq + 1))
                    for t in range(TT):
                        ins = nc.tensor.transpose(misc[:, t * P:(t + 1) * P], xn[:, t, part * P:(part + 1) * P], eye[:])
                elif kind == "qk":
                    w0 = (part % 2) * C + (part // 2) * P
                    for k in range(KC):
                        ins = matmul(misc, wqkv[:, k, w0:w0 + P], xnt[:, k, :], k == 0, k == KC - 1)
                elif kind == "v":
                    for t in range(2):
                        for k in range(KC):
                            tok = (2 * part + t) * P
                            ins = matmul(misc_tiles[:, t, :], xnt[:, k, tok:tok + P], wqkv[:, k, 2 * C:3 * C],
                                         k == 0, k == KC - 1)
                elif kind == "max":
                    pe.wait_ge(neg_ready, seq * NQ + part + 1)
                    for t in range(TT):
                        ins = nc.tensor.transpose(misc[0:2 * QH, t * P:(t + 1) * P], max_in[:, t, :], eye[:])
                elif kind == "heads":
                    pe.wait_ge(heads_t_ready, seq * NQ + part + 1)
                    for t in range(TT):
                        ins = nc.tensor.transpose(misc[:, t * P:(t + 1) * P], heads_t[:, t * P:(t + 1) * P], eye[:])
                elif kind == "turn":
                    for t in range(TT):
                        ins = nc.tensor.transpose(misc[:, t * P:(t + 1) * P], heads[:, t, part * P:(part + 1) * P], eye[:])
                elif kind == "out":
                    for t in range(2):
                        for k in range(KC):
                            tok = (2 * part + t) * P
                            ins = matmul(misc_tiles[:, t, :], att_t[:, k, tok:tok + P], wo[:, k, :], k == 0, k == KC - 1)
                ins.then_inc(filled, 1)

            def scores_for_max(b, local):
                quad, u = (local // STEPS) % NQ, local % STEPS
                seq = b + local // (NQ * STEPS)
                h = quad * QH + u // 2
                if u == 0:
                    pe.wait_ge(aug_done[quad], (seq + 1) * (16 * 8 * QH))
                for i in range(2):
                    tile = 2 * (b * (NQ * STEPS) + local) + i
                    wait(pe, s1_used, tile - 1)
                    t = 2 * (u % 2) + i
                    matmul(ps[:, max_at + i, :], q_aug[0:ROW_MAX, h, t * P:(t + 1) * P], k_aug[0:ROW_MAX, h, :],
                           True, True).then_inc(s1_done, 1)

            def weigh_values(quad_no, quad, kt, seq):
                pe.wait_ge(fixed, quad_no * STEPS + 2 * kt + 2)
                if kt == 0:
                    pe.wait_ge(v_ready, seq * NQ + quad + 1)
                    wait(pe, heads_t_ready, quad_no)
                for g in range(QH):
                    ins = matmul(pv[32 * g:32 * g + 32, :], v_aug[:, kt, quad * QH + g, :], probs[:, kt % 2, g, :],
                                 kt == 0, kt == TT - 1, skip_group_check=True)
                ins.then_inc(pv_done, 1)

            pe.wait_ge(ffn[0]["xnt_ready"], 2 * (B + 1))
            pe.wait_ge(ffn[0]["hid_ready"], FT * B)
            pe.wait_ge(ffn[0]["y_used"], 2 * B)
            pe.wait_ge(aug_in, 16 * 2 * H)
            for name in FILLS_BEFORE[:-1]:
                fill(-1, name)
            for u in range(LEAD):
                scores_for_max(0, u)
            fill(-1, FILLS_BEFORE[-1])

            def turn(b):
                for n in range(NQ):
                    for s in range(STEPS):
                        kt, pair = s // 2, s % 2
                        quad_no = b * NQ + n
                        g = quad_no * STEPS + s
                        if s == 0:
                            pe.wait_ge(max_moved, (quad_no + 1) * (16 * 2 * QH))
                        wait(pe, exp_done, g - 1)
                        for i in range(2):
                            h = n * QH + 2 * pair + i
                            ins = matmul(ps[:, scores_at + 2 * pair + i, :], k_aug[0:ROWS, h, kt * P:(kt + 1) * P],
                                         q_aug[0:ROWS, h, :], True, True)
                        ins.then_inc(st_done, 1)
                        local = n * STEPS + s
                        if not (last(b) and local + LEAD >= NQ * STEPS):
                            scores_for_max(b, local + LEAD)
                        if s == 1 and not (first(b) and n == 0):
                            weigh_values(quad_no - 1, (n - 1) % NQ, TT - 1, b)
                        if s in (3, 5, 7):
                            weigh_values(quad_no, n, (s - 3) // 2, b)
                        name = FILLS.get((n, s))
                        if name in fills_of(b):
                            fill(b, name)

            turns(pe, turn)
            weigh_values(B * NQ - 1, NQ - 1, TT - 1, B - 1)
            for name in TAIL_FILLS:
                fill(B, name)
            pe.wait_ge(drained, fill_no(B, TAIL_FILLS[-1]) + 1)
            turns(pe, lambda b: ffn_turn(1, b))


def kernel(**inputs):
    import concourse.bacc as bacc
    from concourse.bass_utils import run_bass_kernel_spmd

    def laid(a):
        return np.ascontiguousarray(a)

    x = np.asarray(inputs["L0_attn_q"])
    arrays = {
        "x_in": laid(x.reshape(B, TT, P, C).transpose(0, 2, 1, 3)).reshape(B, P, TT * C),
        "w_gate_up": laid(np.concatenate([np.asarray(inputs["L0_ffn_w_gate"]).T,
                                          np.asarray(inputs["L0_ffn_w_up"]).T], axis=1)),
        "w_down": laid(np.asarray(inputs["L0_ffn_w_down"]).T),
        "w_qkv": laid(np.concatenate([np.asarray(inputs[f"L0_attn_W{n}"]).T for n in "qkv"], axis=1)),
        "w_out": laid(np.asarray(inputs["L0_attn_Wo"]).T),
        "b_out": laid(np.asarray(inputs["L0_attn_bo"]).reshape(1, C)),
        **tables(),
    }
    nc = bacc.Bacc("TRN2", target_bir_lowering=False, num_devices=1)
    args = [nc.dram_tensor(n, a.shape, mybir.dt.from_np(a.dtype), kind="ExternalInput").ap() for n, a in arrays.items()]
    args.append(nc.dram_tensor("x_out", (B, P, TT * C), F32, kind="ExternalOutput").ap())
    build_program(nc, *args)
    out = run_bass_kernel_spmd(nc, [arrays], core_ids=[0]).results[0]["x_out"]
    return laid(out.reshape(B, P, TT, C).transpose(0, 2, 1, 3)).reshape(B, L, C)
```

```python
from contextlib import ExitStack

import numpy as np

import concourse.bass as bass
from concourse import mybir

F32 = mybir.dt.float32
F32R = mybir.dt.float32r
I32 = mybir.dt.int32
ALU = mybir.AluOpType
ACT = mybir.ActivationFunctionType

P = 128
B, L, C = 8, 512, 256
H, D = 16, 16
FF = 768
TT = L // P
KC = C // P
FT = FF // P
QH = 4
NQ = H // QH
STEPS = 2 * TT
LEAD = 12
SEG = 64
NSEG = L // SEG
ROW_BIAS = 4 * D
ROW_MAX = ROW_BIAS + 4 * NSEG
ROWS = ROW_MAX + 2
DEQ = float(np.float32(1.0 / 127.0))
EXACT = 4096.0
EPS = 1e-5
MAGIC = float(0x5F3759DF)
NEWTON = 3
LN_OPS = 4 + 4 + 3 + 3 * NEWTON


def slopes():
    start = 2.0 ** (-2.0 ** (-(np.log2(H) - 3)))
    return np.array([start * start ** i for i in range(H)], dtype=np.float32)


def hi_lo(a):
    a = np.asarray(a, np.float32)
    u = a.view(np.uint32)
    hi = ((u + 0x7FF + ((u >> 12) & 1)) & np.uint32(0xFFFFF000)).view(np.float32)
    return hi, a - hi


def tables():
    s = slopes()
    pos = np.arange(L, dtype=np.float64)
    centre = SEG * np.arange(NSEG) + (SEG - 1) / 2
    inside = (np.arange(L)[None, :] // SEG) == np.arange(NSEG)[:, None]
    one = inside.astype(np.float32)
    off = np.where(inside, pos[None, :] - centre[:, None], 0.0).astype(np.float32)
    qb = np.zeros((4 * NSEG, H, L), np.float32)
    for h in range(H):
        a_hi, a_lo = hi_lo(one * s[h])
        b_hi, b_lo = hi_lo(off * s[h])
        qb[:, h] = np.concatenate([a_hi, a_lo, b_hi, b_lo])
    dist = (-np.abs(pos[None, :] - centre[:, None])).astype(np.float32)
    sign = np.sign(pos[None, :] - centre[:, None]).astype(np.float32)
    kb = np.concatenate([dist, dist, sign, sign, np.ones((2, L), np.float32)])
    j, i = np.arange(P)[:, None], np.arange(P)[None, :]
    t = SEG * (i // SEG) + (SEG - 1) / 2
    over = (i // SEG == j // SEG) & ((i > t) == (j > t)) & (np.abs(i - t) > np.abs(j - t))
    excess = np.where(over, 2.0 * np.abs(i - j), 0.0)
    diag = np.exp(-s.astype(np.float64)[None, :, None] * excess[:, None, :]).astype(np.float32)
    return {"q_bias": qb, "k_bias": kb, "diag_table": diag, "eye_table": np.eye(P, dtype=np.float32)}


FILLS = {
    (0, 3): "heads3_prev", (0, 4): "xt0_next", (0, 5): "max1", (0, 6): "xt1_next", (0, 7): "qk0_next",
    (1, 0): "qk1_next", (1, 2): "qk2_next", (1, 3): "heads0", (1, 4): "qk3_next", (1, 5): "max2",
    (1, 6): "v0_next", (1, 7): "turn1_prev",
    (2, 0): "v1_next", (2, 1): "out0_prev", (2, 2): "out1_prev", (2, 3): "heads1", (2, 5): "max3",
    (2, 6): "turn0",
    (3, 3): "heads2", (3, 5): "max0_next",
}
ALL_FILLS = list(FILLS.values())
FILLS_BEFORE = ["qk0_next", "qk1_next", "qk2_next", "qk3_next", "v0_next", "v1_next", "max0_next"]
FIRST_FILLS = [f for f in ALL_FILLS if not f.endswith("_prev")]
LAST_FILLS = [f for f in ALL_FILLS if not f.endswith("_next") or f.startswith("xt")]
TAIL_FILLS = ["heads3_prev", "turn1_prev", "out0_prev", "out1_prev"]


def fill_no(b, name):
    if isinstance(b, int):
        if b < 0:
            return FILLS_BEFORE.index(name)
        if b == 0:
            return len(FILLS_BEFORE) + FIRST_FILLS.index(name)
        if b >= B - 1:
            until = len(FILLS_BEFORE) + len(FIRST_FILLS) + (B - 2) * len(ALL_FILLS)
            if b == B - 1:
                return until + LAST_FILLS.index(name)
            return until + len(LAST_FILLS) + TAIL_FILLS.index(name)
    return b * len(ALL_FILLS) + (
        len(FILLS_BEFORE) + len(FIRST_FILLS) - len(ALL_FILLS) + ALL_FILLS.index(name))


HI_KINDS = ("xt", "qk", "turn")


def hi_no(b, name):
    def of(fills):
        return [f for f in fills if f.startswith(HI_KINDS)]

    before, firsts, mids, lasts, tails = map(of, (FILLS_BEFORE, FIRST_FILLS, ALL_FILLS, LAST_FILLS, TAIL_FILLS))
    if isinstance(b, int):
        if b < 0:
            return before.index(name)
        if b == 0:
            return len(before) + firsts.index(name)
        if b >= B - 1:
            until = len(before) + len(firsts) + (B - 2) * len(mids)
            return until + (lasts.index(name) if b == B - 1 else len(lasts) + tails.index(name))
    return b * len(mids) + (len(before) + len(firsts) - len(mids) + mids.index(name))


def build_program(nc, d_x, d_wgu, d_wdn, d_watt, d_bo, d_qb, d_kb, d_diag, d_eye, d_out):
    d_parts = nc.dram_tensor("parts_scratch", (2, P, 2 * 2 * L), F32).ap()
    with ExitStack() as ctx:
        def sem(name):
            return ctx.enter_context(nc.semaphore(name))

        cursor = [-(-nc.sbuf_base // 32) * 32]

        def sb(name, shape, dt=F32, at=None):
            size = 4 * int(np.prod(shape[1:]))
            offset = cursor[0] if at is None else at
            if at is None:
                cursor[0] += -(-size // 32) * 32
            assert offset + size <= nc.sbuf_usable_end
            return nc.alloc_sbuf_tensor_at(name, shape, dt, offset=offset)

        def here():
            return cursor[0]

        x_sb = sb("x_sb", [P, B * TT * C])
        wgu_r = sb("wgu_r", [P, KC, 2 * FF], F32R, at=here())
        wgu = sb("wgu", [P, KC, 2 * FF])
        wdn_r = sb("wdn_r", [P, FT, C], F32R, at=here())
        wdn = sb("wdn", [P, FT, C])
        wqkv = sb("wqkv", [P, 2, KC, 3 * C], F32R)
        wo = sb("wo", [P, 2, KC, C], F32R)
        bo = sb("bo", [P, C])
        eye = sb("eye", [P, P])
        diag = sb("diag", [P, H, P])
        q_aug = sb("q_aug", [P, H, L], F32R)
        wgu_i = sb("wgu_i", [P, KC, 2 * FF], I32, at=here())
        wdn_i = sb("wdn_i", [P, FT, C], I32, at=here() + 4 * KC * 2 * FF)
        k_aug = sb("k_aug", [P, H, L], F32R)
        v_aug = sb("v_aug", [P, TT, H, 2 * D])
        xn = sb("xn", [P, TT, C])
        xnt = sb("xnt", [P, 2, KC, L], F32R)
        row_max = sb("row_max", [P, 2, TT, QH])
        max_in = sb("max_in", [P, TT, 2 * QH])
        den = sb("den", [P, TT, QH, 1])
        stats = sb("stats", [P, TT, 6])
        mean_var = sb("mean_var", [P, TT, 2])
        var = sb("var", [P, TT])
        rstd = sb("rstd", [P, TT])
        newton = sb("newton", [P, TT])
        w_max = sb("w_max", [P, 3])
        w_top = sb("w_top", [P, 1])
        beyond = sb("beyond", [P, 1], I32)
        own = here()
        hid = sb("hid", [P, 2, L])
        hid_r = sb("hid_r", [P, 2, FT, L], F32R)
        gated = sb("gated", [P, 2, L])
        w_att = sb("w_att", [P, KC, 4 * C])
        cursor[0] = own
        probs = sb("probs", [P, 2, QH, L])
        parts = sb("parts", [P, 2, 2, 2, L], F32R)
        v_new = sb("v_new", [P, TT, C])
        heads_t = sb("heads_t", [P, L])
        heads = sb("heads", [P, TT, C])
        att_t = sb("att_t", [P, 2, KC, L], F32R)
        max_row = sb("max_row", [2 * QH, L], F32R)

        ps = ctx.enter_context(nc.psum_tensor("ps", [P, 8, L], F32))
        scores_at, max_at, pv, misc = 0, 4, ps[:, 6, :], ps[:, 7, :]
        gate_at, up_at, turn_at, y_at = 0, 2, 4, 6
        misc_tiles = misc.rearrange("p (t c) -> p t c", t=2)

        x_in = [sem(f"x_loaded{b}") for b in range(B)]
        gu_in, dn_in, eye_in, watt_in, att_in, aug_in, stored = (
            sem(n) for n in ("gu_in", "dn_in", "eye_in", "watt_in", "att_in", "aug_in", "stored"))
        w_ready, w_seen, w_reduced, beyond_ready = (sem(n) for n in ("w_ready", "w_seen", "w_reduced", "beyond_ready"))
        watt_hi, watt_ready, w_general = sem("watt_hi"), sem("watt_ready"), sem("w_general")
        ln_step, xn_ready = sem("ln_step"), sem("xn_ready")
        ffn = [{n: sem(f"{n}_{w}") for n in ("turned", "xnt_ready", "gate_done", "up_done", "gated_ready",
                                             "hid_ready", "hid_hi", "hid_lo", "xnt_hi", "y_done", "y_used")} for w in ("a", "c")]
        ones_set, bo_added = sem("ones_set"), sem("bo_added")
        filled, drained, hi_ready = sem("filled"), sem("drained"), sem("hi_ready")
        s1_done, s1_used = sem("s1_done"), sem("s1_used")
        neg_hi, neg_ready = sem("neg_hi"), sem("neg_ready")
        aug_done = [sem(f"aug_done{n}") for n in range(NQ)]
        parts_out = sem("parts_out")
        max_moved = sem("max_moved")
        st_done, exp_done, fixed = sem("st_done"), sem("exp_done"), sem("fixed")
        pv_done, heads_t_ready, den_ready, v_ready = (sem(n) for n in ("pv_done", "heads_t_ready", "den_ready", "v_ready"))
        block = ctx.enter_context(nc.Block())

        def wait(eng, s, value):
            if not (isinstance(value, int) and value <= 0):
                eng.wait_ge(s, value)

        def turns(eng, body):
            body(0)
            with eng.Fori(1, B - 1) as b:
                body(b)
            body(B - 1)

        def first(b):
            return isinstance(b, int) and b == 0

        def last(b):
            return isinstance(b, int) and b == B - 1

        def fills_of(b):
            return FIRST_FILLS if first(b) else LAST_FILLS if last(b) else ALL_FILLS

        def x_of(b, tile, n=1):
            at = b * (TT * C) + tile * C
            return x_sb[:, bass.ds(at, n * C)]

        def fill_parts(b, name):
            base = name.split("_")[0]
            seq = b + 1 if name.endswith("_next") else b - 1 if name.endswith("_prev") else b
            return seq, base[:-1], int(base[-1])

        @block.sync
        def _(sp):
            sp.dma_start(x_sb[:, 0:TT * C], d_x[0]).then_inc(x_in[0], 16)
            sp.dma_start(wgu_i[:], d_wgu.rearrange("(k p) n -> p k n", p=P)).then_inc(gu_in, 16)
            sp.dma_start(eye[:], d_eye).then_inc(eye_in, 16)
            sp.dma_start(wdn_i[:], d_wdn.rearrange("(k p) n -> p k n", p=P)).then_inc(dn_in, 16)
            for b in range(1, B):
                sp.dma_start(x_sb[:, b * TT * C:(b + 1) * TT * C], d_x[b]).then_inc(x_in[b], 16)
                if b == 1:
                    sp.dma_start(w_att[:], d_watt.rearrange("(k p) n -> p k n", p=P)).then_inc(watt_in, 16)
            sp.dma_start(bo[:], d_bo.to_broadcast([P, C])).then_inc(att_in, 16)
            sp.dma_start(diag[:], d_diag).then_inc(att_in, 16)

            def put_parts(half):
                sp.dma_start(d_parts[half], parts[:, half, :, :, :].rearrange("p a b t -> p (a b t)").bitcast(F32)
                             ).then_inc(parts_out, 16)

            def get_rows(quad, count):
                sp.wait_ge(parts_out, 16 * count)
                half = quad // 2
                these = slice(QH * (quad % 2), QH * (quad % 2 + 1))
                for rep in range(2):
                    for part in range(2):
                        for is_k, aug, r in ((0, q_aug, (2 * rep + part) * D), (1, k_aug, (2 * part + rep) * D)):
                            src = d_parts[half].rearrange("(h d) (a b t) -> d h a b t", d=D, a=2, b=2)
                            sp.dma_start(aug[r:r + D, quad * QH:(quad + 1) * QH, :].bitcast(F32),
                                         src[:, these, is_k, part, :]).then_inc(aug_done[quad], 16)

            def move_max(quad, made):
                sp.wait_ge(drained, made + 1)
                for part in range(2):
                    sp.dma_start(q_aug[ROW_MAX + part:ROW_MAX + part + 1, quad * QH:(quad + 1) * QH, :].bitcast(F32),
                                 max_row[part * QH:(part + 1) * QH, :].bitcast(F32)).then_inc(max_moved, 16)

            for half in range(2):
                sp.wait_ge(drained, fill_no(-1, f"qk{2 * half + 1}_next") + 1)
                put_parts(half)
                for quad in (2 * half, 2 * half + 1):
                    get_rows(quad, half + 1)
            move_max(0, fill_no(-1, "max0_next"))

            def turn(b):
                for n in range(NQ):
                    if n + 1 < NQ:
                        move_max(n + 1, fill_no(b, f"max{n + 1}"))
                    elif not last(b):
                        move_max(0, fill_no(b, "max0_next"))
                    if not last(b):
                        steps = STEPS + 4 if n == 0 else (n + 1) * STEPS
                        sp.wait_ge(st_done, b * (NQ * STEPS) + steps)
                        if n < 2:
                            put_parts(n)
                        get_rows(n, 2 * b + (3 if n == 0 else 4))

            turns(sp, turn)

            def store(b):
                sp.wait_ge(ffn[1]["y_used"], 2 * b + 2)
                sp.dma_start(d_out[b], x_of(b, 0, TT)).then_inc(stored, 16)
            for b in range(B):
                store(b)
            sp.wait_ge(stored, 16 * B)

        @block.gpsimd
        def _(pool):
            pool.wait_ge(w_seen, 3)
            nc.gpsimd.partition_all_reduce(w_top[:, :], w_max[:, 2:3], P, bass.bass_isa.ReduceOp.max).then_inc(w_reduced, 1)
            pool.wait_ge(w_ready, 2)
            pool.wait_ge(watt_ready, 1)
            pool.dma_start(q_aug[ROW_BIAS:ROW_MAX, :, :], d_qb).then_inc(aug_in, 16)
            pool.dma_start(k_aug[ROW_BIAS:ROWS, :, :],
                           d_kb.rearrange("r (o t) -> r o t", o=1).to_broadcast([ROWS - ROW_BIAS, H, L])
                           ).then_inc(aug_in, 16)
            nc.gpsimd.memset(v_aug[:], 1.0).then_inc(ones_set, 1)
            pool.wait_ge(ones_set, 1)

            def split_hidden(w, b):
                s = ffn[w]
                for f in range(FT):
                    pool.wait_ge(s["hid_hi"], FT * b + f + 1)
                    nc.gpsimd.tensor_tensor(hid_r[:, 1, f, :], hid[:, f % 2, :], hid_r[:, 0, f, :].bitcast(F32),
                                            ALU.subtract).then_inc(s["hid_lo"], 1)

            turns(pool, lambda b: split_hidden(0, b))

            def place_v(b, quad):
                nc.gpsimd.tensor_copy(
                    v_aug[:, :, quad * QH:(quad + 1) * QH, 0:D],
                    v_new[:, :, quad * QH * D:(quad + 1) * QH * D].rearrange("p t (g d) -> p t g d", g=QH),
                ).then_inc(v_ready, 1)

            pool.wait_ge(drained, fill_no(-1, "v1_next") + 1)
            for quad in range(3):
                place_v(0, quad)
            pool.wait_ge(att_in, 16 * 2)

            def add_bo(b):
                pool.wait_ge(xn_ready, TT * (B + b) + TT)
                for tile in range(TT):
                    nc.gpsimd.tensor_tensor(x_of(b, tile), x_of(b, tile), bo[:], ALU.add).then_inc(bo_added, 1)

            add_bo(0)

            def turn(b):
                for n in range(NQ):
                    for s in range(STEPS):
                        kt, pair = s // 2, s % 2
                        g = b * (NQ * STEPS) + n * STEPS + s
                        if (n, s) == (0, 3) and not first(b):
                            pool.wait_ge(pv_done, b * (NQ * TT))
                        if (n, s) == (2, 4) and not last(b):
                            pool.wait_ge(pv_done, b * (NQ * TT) + 2 * TT)
                            pool.wait_ge(drained, fill_no(b, "v1_next") + 1)
                        if (n, s) == (3, 4) and not last(b):
                            pool.wait_ge(pv_done, b * (NQ * TT) + 3 * TT)
                        pool.wait_ge(exp_done, g + 1)
                        tile = probs[:, kt % 2, 2 * pair:2 * pair + 2, kt * P:(kt + 1) * P]
                        nc.gpsimd.tensor_tensor(tile, tile, diag[:, n * QH + 2 * pair:n * QH + 2 * pair + 2, :],
                                                ALU.mult).then_inc(fixed, 1)
                        if (n, s) == (0, 3):
                            place_v(b, 3)
                        if not last(b):
                            if (n, s) == (1, 0):
                                add_bo(b + 1)
                            if (n, s) == (2, 4):
                                place_v(b + 1, 0)
                                place_v(b + 1, 1)
                            if (n, s) == (3, 4):
                                place_v(b + 1, 2)

            turns(pool, turn)
            turns(pool, lambda b: split_hidden(1, b))

        @block.scalar
        def _(act):
            def ffn_turn(w, b):
                s = ffn[w]

                def hidden_hi(f):
                    act.wait_ge(s["hid_ready"], FT * b + f + 1)
                    if f == 0:
                        wait(act, s["y_done"], 2 * b)
                    nc.scalar.copy(hid_r[:, 0, f, :], hid[:, f % 2, :]).then_inc(s["hid_hi"], 1)

                for f in range(FT):
                    act.wait_ge(s["gate_done"], FT * b + f + 1)
                    wait(act, s["hid_ready"], FT * b + f - 1)
                    nc.scalar.activation(gated[:, f % 2, :], ps[:, gate_at + f % 2, :], ACT.Silu, scale=DEQ
                                         ).then_inc(s["gated_ready"], 1)
                    if f >= 1:
                        hidden_hi(f - 1)
                hidden_hi(FT - 1)
                if not (w == 1 and last(b)):
                    turned(w, b + 1)

            def turned(w, b):
                s = ffn[w]
                for k in range(KC):
                    act.wait_ge(s["turned"], 2 * b + k + 1 - 2 * w)
                    nc.scalar.copy(xnt[:, 0, k, :], ps[:, turn_at + k, :]).then_inc(s["xnt_hi"], 1)

            act.wait_ge(dn_in, 16)
            nc.scalar.copy(wdn_r[:], wdn_i[:]).then_inc(w_ready, 1)
            turned(0, 0)
            act.wait_ge(watt_in, 16)
            nc.scalar.copy(wqkv[:, 0, :, :], w_att[:, :, 0:3 * C]).then_inc(watt_hi, 1)
            nc.scalar.copy(wo[:, 0, :, :], w_att[:, :, 3 * C:4 * C]).then_inc(watt_hi, 1)
            turns(act, lambda b: ffn_turn(0, b))

            def drain(b, name):
                at = fill_no(b, name)
                seq, kind, part = fill_parts(b, name)
                if kind in ("heads", "out"):
                    return
                act.wait_ge(filled, at + 1)
                if kind == "xt":
                    nc.scalar.copy(xnt[:, 0, part, :], misc).then_inc(hi_ready, 1)
                elif kind == "qk":
                    half, is_k = part // 2, part % 2
                    if not (isinstance(seq, int) and seq == 0):
                        act.wait_ge(parts_out, 16 * 2 * seq)
                    nc.scalar.activation(parts[:, half, is_k, 0, :], misc, ACT.Copy,
                                         scale=1.0 if is_k else D ** -0.5).then_inc(hi_ready, 1)
                elif kind == "v":
                    if not (isinstance(seq, int) and seq == 0):
                        act.wait_ge(v_ready, NQ * seq)
                    nc.scalar.copy(v_new[:, 2 * part:2 * part + 2, :], misc_tiles).then_inc(drained, 1)
                elif kind == "max":
                    quad_no = seq * NQ + part
                    wait(act, max_moved, quad_no * (16 * 2))
                    nc.scalar.copy(max_row[:, :], misc[0:2 * QH, :]).then_inc(drained, 1)
                elif kind == "turn":
                    nc.scalar.copy(att_t[:, 0, part, :], misc).then_inc(hi_ready, 1)

            for name in FILLS_BEFORE:
                drain(-1, name)

            def take_heads(quad_no):
                act.wait_ge(pv_done, (quad_no + 1) * TT)
                nc.scalar.copy(heads_t[:, :], pv).then_inc(heads_t_ready, 1)

            def turn(b):
                for n in range(NQ):
                    for s in range(STEPS):
                        kt, pair = s // 2, s % 2
                        quad_no = b * NQ + n
                        g = quad_no * STEPS + s
                        act.wait_ge(st_done, g + 1)
                        wait(act, pv_done, quad_no * TT + kt - 1)
                        at = scores_at + 2 * pair
                        nc.scalar.activation(probs[:, kt % 2, 2 * pair:2 * pair + 2, :], ps[:, at:at + 2, :],
                                             ACT.Exp).then_inc(exp_done, 1)
                        if s == 2 and not (first(b) and n == 0):
                            take_heads(quad_no - 1)
                        name = FILLS.get((n, s))
                        if name in fills_of(b):
                            drain(b, name)

            turns(act, turn)
            take_heads(B * NQ - 1)
            for name in TAIL_FILLS:
                drain(B, name)
            turns(act, lambda b: ffn_turn(1, b))

        @block.vector
        def _(dve):
            def ln_stats(no, b, tile):
                nc.vector.bn_stats(stats[:, tile, :], x_of(b, tile)).then_inc(ln_step, 1)

            def ln_finish(no, b):
                k = [no * LN_OPS + TT]

                def link(ins):
                    ins.then_inc(ln_step, 1)
                    k[0] += 1 if isinstance(k[0], int) else 0
                    k[0] = k[0] if isinstance(k[0], int) else k[0] + 1
                    dve.wait_ge(ln_step, k[0])

                for tile in range(TT):
                    ins = nc.vector.bn_aggr(mean_var[:, tile, :], stats[:, tile, :])
                    if tile < TT - 1:
                        ins.then_inc(ln_step, 1)
                        k[0] = k[0] + 1
                link(ins)
                link(nc.vector.tensor_scalar(var[:, :], mean_var[:, :, 1], EPS, None, ALU.add))
                link(nc.vector.tensor_scalar(rstd[:, :].bitcast(I32), var[:, :].bitcast(I32), 1, None,
                                             ALU.logical_shift_right))
                link(nc.vector.tensor_scalar(rstd[:, :].bitcast(I32), rstd[:, :].bitcast(I32), -1.0, MAGIC,
                                             ALU.mult, ALU.add))
                for _ in range(NEWTON):
                    link(nc.vector.scalar_tensor_tensor(newton[:, :], rstd[:, :], -0.5, rstd[:, :],
                                                        ALU.mult, ALU.mult))
                    link(nc.vector.tensor_tensor(newton[:, :], newton[:, :], var[:, :], ALU.mult))
                    link(nc.vector.scalar_tensor_tensor(rstd[:, :], newton[:, :], 1.5, rstd[:, :],
                                                        ALU.add, ALU.mult))
                for tile in range(TT):
                    nc.vector.tensor_scalar(xn[:, tile, :], x_of(b, tile), mean_var[:, tile, 0:1],
                                            rstd[:, tile:tile + 1], ALU.subtract, ALU.mult).then_inc(xn_ready, 1)

            def stats_ready(no):
                dve.wait_ge(ln_step, no * LN_OPS + TT)

            def turned(w, b):
                s = ffn[w]
                for k in range(KC):
                    dve.wait_ge(s["xnt_hi"], 2 * b + k + 1 - 2 * w)
                    nc.vector.tensor_tensor(xnt[:, 1, k, :], ps[:, turn_at + k, :], xnt[:, 0, k, :].bitcast(F32),
                                            ALU.subtract).then_inc(s["xnt_ready"], 1)

            def ffn_turn(w, b):
                s = ffn[w]
                then = (2 * w * B + b + 1, b + 1) if not last(b) else (B, 0) if w == 0 else None
                for f in range(FT):
                    dve.wait_ge(s["gated_ready"], FT * b + f + 1)
                    dve.wait_ge(s["up_done"], FT * b + f + 1)
                    wait(dve, s["hid_lo"], FT * b + f - 1)
                    if then and f == 3:
                        stats_ready(then[0])
                        wait(dve, s["turned"], 2 * b + 2 - 2 * w)
                    nc.vector.scalar_tensor_tensor(hid[:, f % 2, :], ps[:, up_at + f % 2, :], DEQ, gated[:, f % 2, :],
                                                   ALU.mult, ALU.mult).then_inc(s["hid_ready"], 1)
                    if then and f == 2:
                        if last(b):
                            dve.wait_ge(s["y_used"], 2)
                        for tile in range(TT):
                            ln_stats(*then, tile)
                    if then and f == 3:
                        ln_finish(*then)
                if not (w == 1 and last(b)):
                    turned(w, b + 1)
                for j in range(2):
                    dve.wait_ge(s["y_done"], 2 * b + j + 1)
                    nc.vector.scalar_tensor_tensor(x_of(b, 2 * j, 2), ps[:, y_at + j, :], 0.5 * DEQ, x_of(b, 2 * j, 2),
                                                   ALU.mult, ALU.add).then_inc(s["y_used"], 1)

            dve.wait_ge(x_in[0], 16)
            for tile in range(TT):
                ln_stats(0, 0, tile)
            stats_ready(0)
            ln_finish(0, 0)
            dve.wait_ge(gu_in, 16)
            nc.vector.tensor_copy(wgu_r[:], wgu_i[:]).then_inc(w_ready, 1)
            nc.vector.tensor_reduce(w_max[:, 0:1], wgu_i[:].rearrange("p k n -> p (k n)"), mybir.AxisListType.X,
                                    ALU.max, apply_absolute_value=True).then_inc(w_seen, 1)
            dve.wait_ge(dn_in, 16)
            nc.vector.tensor_reduce(w_max[:, 1:2], wdn_i[:].rearrange("p k n -> p (k n)"), mybir.AxisListType.X,
                                    ALU.max, apply_absolute_value=True).then_inc(w_seen, 1)
            dve.wait_ge(w_seen, 2)
            nc.vector.tensor_tensor(w_max[:, 2:3], w_max[:, 0:1], w_max[:, 1:2], ALU.max).then_inc(w_seen, 1)
            turned(0, 0)
            dve.wait_ge(w_reduced, 1)
            nc.vector.tensor_scalar(beyond[:, :], w_top[:, :], EXACT, None, ALU.is_gt).then_inc(beyond_ready, 1)
            dve.wait_ge(beyond_ready, 1)
            with dve.If(dve.value_load(beyond[0:1, 0:1], min_val=0, max_val=1) != 0):
                dve.wait_ge(w_ready, 2)
                nc.vector.tensor_copy(wgu[:], wgu_i[:]).then_inc(w_general, 1)
                nc.vector.tensor_copy(wdn[:], wdn_i[:]).then_inc(w_general, 1)
            dve.wait_ge(watt_hi, 2)
            nc.vector.tensor_tensor(wqkv[:, 1, :, :], w_att[:, :, 0:3 * C], wqkv[:, 0, :, :].bitcast(F32),
                                    ALU.subtract).then_inc(watt_ready, 1)
            nc.vector.tensor_tensor(wo[:, 1, :, :], w_att[:, :, 3 * C:4 * C], wo[:, 0, :, :].bitcast(F32),
                                    ALU.subtract).then_inc(watt_ready, 1)
            for b in range(1, B):
                dve.wait_ge(x_in[b], 16)
            turns(dve, lambda b: ffn_turn(0, b))
            dve.wait_ge(ffn[0]["y_used"], 2 * B)

            def row_maxima(unit):
                u = unit[1]
                for i in range(2):
                    dve.wait_ge(s1_done, unit[0] + i + 1)
                    nc.vector.reduce_max(row_max[:, unit[2], 2 * (u % 2) + i, u // 2:u // 2 + 1],
                                         ps[:, max_at + i, :], mybir.AxisListType.X).then_inc(s1_used, 1)

            def unit_at(b, local):
                return 2 * (b * (NQ * STEPS) + local), local % STEPS, (local // STEPS) % 2

            def negate(quad_no, slot):
                dve.wait_ge(s1_used, (quad_no + 1) * (2 * STEPS))
                m = row_max[:, slot, :, :]
                nc.vector.tensor_scalar(max_in[:, :, 0:QH].bitcast(F32R), m, -1.0, None, ALU.mult).then_inc(neg_hi, 1)
                dve.wait_ge(neg_hi, quad_no + 1)
                nc.vector.scalar_tensor_tensor(max_in[:, :, QH:2 * QH], m, -1.0, max_in[:, :, 0:QH],
                                               ALU.mult, ALU.subtract).then_inc(neg_ready, 1)

            def drain(b, name):
                at = fill_no(b, name)
                seq, kind, part = fill_parts(b, name)
                if kind in HI_KINDS:
                    dve.wait_ge(hi_ready, hi_no(b, name) + 1)
                if kind in ("xt", "turn"):
                    to = xnt if kind == "xt" else att_t
                    nc.vector.tensor_tensor(to[:, 1, part, :], misc, to[:, 0, part, :].bitcast(F32),
                                            ALU.subtract).then_inc(drained, 1)
                elif kind == "qk":
                    half, is_k = part // 2, part % 2
                    nc.vector.scalar_tensor_tensor(parts[:, half, is_k, 1, :], misc, 1.0 if is_k else D ** -0.5,
                                                   parts[:, half, is_k, 0, :].bitcast(F32),
                                                   ALU.mult, ALU.subtract).then_inc(drained, 1)
                elif kind == "heads":
                    dve.wait_ge(filled, at + 1)
                    got = misc.rearrange("p (t g d) -> p t g d", t=TT, g=QH)
                    nc.vector.reciprocal(den[:, :, :, :], got[:, :, :, D:D + 1]).then_inc(den_ready, 1)
                    dve.wait_ge(den_ready, seq * NQ + part + 1)
                    nc.vector.tensor_tensor(
                        heads[:, :, part * QH * D:(part + 1) * QH * D].rearrange("p t (g d) -> p t g d", g=QH),
                        got[:, :, :, 0:D], den[:, :, :, :].to_broadcast([P, TT, QH, D]), ALU.mult
                    ).then_inc(drained, 1)
                elif kind == "out":
                    dve.wait_ge(filled, at + 1)
                    dve.wait_ge(bo_added, TT * (seq + 1))
                    xs = x_of(seq, 2 * part, 2)
                    nc.vector.tensor_tensor(xs, misc, xs, ALU.add).then_inc(drained, 1)

            for name in FILLS_BEFORE[:-1]:
                drain(-1, name)
            for u in range(LEAD):
                row_maxima(unit_at(0, u))
                if u == STEPS - 1:
                    negate(0, 0)

            def turn(b):
                then = (2 * B, 0) if last(b) else (B + b + 1, b + 1)
                for n in range(NQ):
                    for s in range(STEPS):
                        local = n * STEPS + s
                        if n == 0 and s < 4:
                            if last(b) and s == 0:
                                dve.wait_ge(drained, fill_no(1, "out1_prev") + 1)
                            ln_stats(*then, s)
                        if (n, s) == (0, 3):
                            stats_ready(then[0])
                        if not (last(b) and local + LEAD >= NQ * STEPS):
                            row_maxima(unit_at(b, local + LEAD))
                        if s == 4 and not (last(b) and n == NQ - 1):
                            negate(b * NQ + n + 1, (n + 1) % 2)
                        if (n, s) == (0, 3):
                            ln_finish(*then)
                        name = FILLS.get((n, s))
                        if name in fills_of(b):
                            drain(b, name)

            turns(dve, turn)
            for name in TAIL_FILLS:
                drain(B, name)
            dve.wait_ge(drained, fill_no(B, TAIL_FILLS[-1]) + 1)
            turns(dve, lambda b: ffn_turn(1, b))

        @block.tensor
        def _(pe):
            def matmul(out, lhs, rhs, start, stop, **k):
                return nc.tensor.matmul(out, lhs, rhs, start=start, stop=stop, **k)

            def turn_x(w, b):
                s = ffn[w]
                pe.wait_ge(xn_ready, TT * (2 * w * B + b + 1))
                if w == 1:
                    wait(pe, s["xnt_ready"], 2 * b - 2)
                else:
                    wait(pe, s["xnt_ready"], 2 * b)
                for k in range(KC):
                    for t in range(TT):
                        ins = nc.tensor.transpose(ps[:, turn_at + k, t * P:(t + 1) * P],
                                                  xn[:, t, k * P:(k + 1) * P], eye[:])
                    ins.then_inc(s["turned"], 1)

            def ffn_turn(w, b):
                s = ffn[w]
                if w == 0:
                    pe.wait_ge(s["xnt_ready"], 2 * b + 2)
                else:
                    wait(pe, s["xnt_ready"], 2 * b)
                either(lambda weights, r: gate_up(weights[0], r, s, b))
                if not (w == 1 and last(b)):
                    turn_x(w, b + 1)
                wait(pe, s["y_used"], 2 * b)
                either(lambda weights, r: down(weights[1], r, s, b))

            def either(products):
                with pe.If(general != 0):
                    pe.wait_ge(w_general, 2)
                    products((wgu, wdn), F32)
                with pe.Else():
                    products((wgu_r, wdn_r), F32R)

            def gate_up(weights, dtype, s, b):
                for f in range(FT):
                    wait(pe, s["hid_ready"], FT * b + f - 1)
                    for which, at, done in ((0, gate_at, "gate_done"), (1, up_at, "up_done")):
                        w0 = which * FF + f * P
                        for k in range(KC):
                            for part in range(2):
                                moving = xnt[:, part, k, :]
                                ins = matmul(ps[:, at + f % 2, :], weights[:, k, w0:w0 + P],
                                             moving if dtype == F32R else moving.bitcast(F32),
                                             k == 0 and part == 0, k == KC - 1 and part == 1)
                        ins.then_inc(s[done], 1)

            def down(weights, dtype, s, b):
                for f in range(FT):
                    for part in range(2):
                        pe.wait_ge(s["hid_lo" if part else "hid_hi"], FT * b + f + 1)
                        for t in range(TT):
                            out = ps[:, y_at + t // 2, (t % 2) * C:(t % 2 + 1) * C]
                            tokens = hid_r[:, part, f, t * P:(t + 1) * P]
                            ins = matmul(out, tokens if dtype == F32R else tokens.bitcast(F32), weights[:, f, :],
                                         f == 0 and part == 0 and t % 2 == 0, f == FT - 1 and part == 1,
                                         skip_group_check=True)
                            if f == FT - 1 and part == 1 and t % 2 == 1:
                                ins.then_inc(s["y_done"], 1)

            pe.wait_ge(eye_in, 16)
            turn_x(0, 0)
            pe.wait_ge(w_ready, 2)
            pe.wait_ge(beyond_ready, 1)
            general = pe.value_load(beyond[0:1, 0:1], min_val=0, max_val=1)
            turns(pe, lambda b: ffn_turn(0, b))

            def split_products(out, lhs, lhs_at, rhs, rhs_at):
                made = [(k, a, c) for k in range(KC) for a, c in ((0, 0), (0, 1), (1, 0))]
                for k, a, c in made:
                    ins = matmul(out, lhs[:, a, k, lhs_at], rhs[:, c, k, rhs_at], (k, a, c) == made[0],
                                 (k, a, c) == made[-1])
                return ins

            def fill(b, name):
                at = fill_no(b, name)
                seq, kind, part = fill_parts(b, name)
                wait(pe, drained, at)
                if kind == "xt":
                    pe.wait_ge(xn_ready, TT * (B + seq + 1))
                    for t in range(TT):
                        ins = nc.tensor.transpose(misc[:, t * P:(t + 1) * P], xn[:, t, part * P:(part + 1) * P], eye[:])
                elif kind == "qk":
                    w0 = (part % 2) * C + (part // 2) * P
                    ins = split_products(misc, wqkv, slice(w0, w0 + P), xnt, slice(0, L))
                elif kind == "v":
                    for t in range(2):
                        tok = (2 * part + t) * P
                        ins = split_products(misc_tiles[:, t, :], xnt, slice(tok, tok + P), wqkv, slice(2 * C, 3 * C))
                elif kind == "max":
                    pe.wait_ge(neg_ready, seq * NQ + part + 1)
                    for t in range(TT):
                        ins = nc.tensor.transpose(misc[0:2 * QH, t * P:(t + 1) * P], max_in[:, t, :], eye[:])
                elif kind == "heads":
                    pe.wait_ge(heads_t_ready, seq * NQ + part + 1)
                    for t in range(TT):
                        ins = nc.tensor.transpose(misc[:, t * P:(t + 1) * P], heads_t[:, t * P:(t + 1) * P], eye[:])
                elif kind == "turn":
                    for t in range(TT):
                        ins = nc.tensor.transpose(misc[:, t * P:(t + 1) * P], heads[:, t, part * P:(part + 1) * P], eye[:])
                elif kind == "out":
                    for t in range(2):
                        tok = (2 * part + t) * P
                        ins = split_products(misc_tiles[:, t, :], att_t, slice(tok, tok + P), wo, slice(0, C))
                ins.then_inc(filled, 1)

            def scores_for_max(b, local):
                quad, u = (local // STEPS) % NQ, local % STEPS
                seq = b + local // (NQ * STEPS)
                h = quad * QH + u // 2
                if u == 0:
                    pe.wait_ge(aug_done[quad], (seq + 1) * (16 * 8))
                for i in range(2):
                    tile = 2 * (b * (NQ * STEPS) + local) + i
                    wait(pe, s1_used, tile - 1)
                    t = 2 * (u % 2) + i
                    matmul(ps[:, max_at + i, :], q_aug[0:ROW_MAX, h, t * P:(t + 1) * P], k_aug[0:ROW_MAX, h, :],
                           True, True).then_inc(s1_done, 1)

            def weigh_values(quad_no, quad, kt, seq):
                pe.wait_ge(fixed, quad_no * STEPS + 2 * kt + 2)
                if kt == 0:
                    pe.wait_ge(v_ready, seq * NQ + quad + 1)
                    wait(pe, heads_t_ready, quad_no)
                for g in range(QH):
                    ins = matmul(pv[32 * g:32 * g + 32, :], v_aug[:, kt, quad * QH + g, :], probs[:, kt % 2, g, :],
                                 kt == 0, kt == TT - 1, skip_group_check=True)
                ins.then_inc(pv_done, 1)

            pe.wait_ge(ffn[0]["xnt_ready"], 2 * (B + 1))
            pe.wait_ge(ffn[0]["hid_ready"], FT * B)
            pe.wait_ge(ffn[0]["y_used"], 2 * B)
            pe.wait_ge(aug_in, 16 * 2)
            pe.wait_ge(watt_ready, 2)
            for name in FILLS_BEFORE[:-1]:
                fill(-1, name)
            for u in range(LEAD):
                scores_for_max(0, u)
            fill(-1, FILLS_BEFORE[-1])

            def turn(b):
                for n in range(NQ):
                    for s in range(STEPS):
                        kt, pair = s // 2, s % 2
                        quad_no = b * NQ + n
                        g = quad_no * STEPS + s
                        if s == 0:
                            pe.wait_ge(max_moved, (quad_no + 1) * (16 * 2))
                        wait(pe, exp_done, g - 1)
                        for i in range(2):
                            h = n * QH + 2 * pair + i
                            ins = matmul(ps[:, scores_at + 2 * pair + i, :], k_aug[0:ROWS, h, kt * P:(kt + 1) * P],
                                         q_aug[0:ROWS, h, :], True, True)
                        ins.then_inc(st_done, 1)
                        local = n * STEPS + s
                        if not (last(b) and local + LEAD >= NQ * STEPS):
                            scores_for_max(b, local + LEAD)
                        if s == 1 and not (first(b) and n == 0):
                            weigh_values(quad_no - 1, (n - 1) % NQ, TT - 1, b)
                        if s in (3, 5, 7):
                            weigh_values(quad_no, n, (s - 3) // 2, b)
                        name = FILLS.get((n, s))
                        if name in fills_of(b):
                            fill(b, name)

            turns(pe, turn)
            weigh_values(B * NQ - 1, NQ - 1, TT - 1, B - 1)
            for name in TAIL_FILLS:
                fill(B, name)
            pe.wait_ge(drained, fill_no(B, TAIL_FILLS[-1]) + 1)
            turns(pe, lambda b: ffn_turn(1, b))


def kernel(**inputs):
    import concourse.bacc as bacc
    from concourse.bass_utils import run_bass_kernel_spmd

    def laid(a):
        return np.ascontiguousarray(a)

    x = np.asarray(inputs["L0_attn_q"])
    arrays = {
        "x_in": laid(x.reshape(B, TT, P, C).transpose(0, 2, 1, 3)).reshape(B, P, TT * C),
        "w_gate_up": laid(np.concatenate([np.asarray(inputs["L0_ffn_w_gate"]).T,
                                          np.asarray(inputs["L0_ffn_w_up"]).T], axis=1)),
        "w_down": laid(np.asarray(inputs["L0_ffn_w_down"]).T),
        "w_att": laid(np.concatenate([np.asarray(inputs[f"L0_attn_W{n}"]).T for n in "qkvo"], axis=1)),
        "b_out": laid(np.asarray(inputs["L0_attn_bo"]).reshape(1, C)),
        **tables(),
    }
    nc = bacc.Bacc("TRN2", target_bir_lowering=False, num_devices=1, dynamic_dma_scratch_size=8192)
    args = [nc.dram_tensor(n, a.shape, mybir.dt.from_np(a.dtype), kind="ExternalInput").ap() for n, a in arrays.items()]
    args.append(nc.dram_tensor("x_out", (B, P, TT * C), F32, kind="ExternalOutput").ap())
    build_program(nc, *args)
    out = run_bass_kernel_spmd(nc, [arrays], core_ids=[0]).results[0]["x_out"]
    return laid(out.reshape(B, P, TT, C).transpose(0, 2, 1, 3)).reshape(B, L, C)
```

```python
from contextlib import ExitStack

import numpy as np

import concourse.bass as bass
from concourse import mybir

F32 = mybir.dt.float32
F32R = mybir.dt.float32r
I32 = mybir.dt.int32
ALU = mybir.AluOpType
ACT = mybir.ActivationFunctionType

P = 128
B, L, C = 8, 512, 256
H, D = 16, 16
FF = 768
TT = L // P
KC = C // P
FT = FF // P
QH = 4
NQ = H // QH
STEPS = 2 * TT
SEG = 64
NSEG = L // SEG
ROW_BIAS = 4 * D
ROW_MAX = ROW_BIAS + 4 * NSEG
ROWS = ROW_MAX + 2
PUTS = 16 * 4
DEQ = float(np.float32(1.0 / 127.0))
EXACT = 4096.0
EPS = 1e-5
MAGIC = float(0x5F3759DF)
NEWTON = 3
LINKS = 3 + 3 * NEWTON
LN_OPS = TT + TT + LINKS


def slopes():
    start = 2.0 ** (-2.0 ** (-(np.log2(H) - 3)))
    return np.array([start * start ** i for i in range(H)], dtype=np.float32)


def hi_lo(a):
    a = np.asarray(a, np.float32)
    u = a.view(np.uint32)
    hi = ((u + 0x7FF + ((u >> 12) & 1)) & np.uint32(0xFFFFF000)).view(np.float32)
    return hi, a - hi


def tables():
    s = slopes()
    pos = np.arange(L, dtype=np.float64)
    centre = SEG * np.arange(NSEG) + (SEG - 1) / 2
    inside = (np.arange(L)[None, :] // SEG) == np.arange(NSEG)[:, None]
    one = inside.astype(np.float32)
    off = np.where(inside, pos[None, :] - centre[:, None], 0.0).astype(np.float32)
    qb = np.zeros((4 * NSEG, H, L), np.float32)
    for h in range(H):
        a_hi, a_lo = hi_lo(one * s[h])
        b_hi, b_lo = hi_lo(off * s[h])
        qb[:, h] = np.concatenate([a_hi, a_lo, b_hi, b_lo])
    dist = (-np.abs(pos[None, :] - centre[:, None])).astype(np.float32)
    sign = np.sign(pos[None, :] - centre[:, None]).astype(np.float32)
    kb = np.concatenate([dist, dist, sign, sign, np.ones((2, L), np.float32)])
    j, i = np.arange(P)[:, None], np.arange(P)[None, :]
    t = SEG * (i // SEG) + (SEG - 1) / 2
    over = (i // SEG == j // SEG) & ((i > t) == (j > t)) & (np.abs(i - t) > np.abs(j - t))
    excess = np.where(over, 2.0 * np.abs(i - j), 0.0)
    diag = np.exp(-s.astype(np.float64)[None, :, None] * excess[:, None, :]).astype(np.float32)
    return {"q_bias": qb, "k_bias": kb, "diag_table": diag, "eye_table": np.eye(P, dtype=np.float32)}


FILLS = {
    (0, 3): "heads3_prev", (0, 5): "max1", (0, 6): "xt0_next", (0, 7): "xt1_next",
    (1, 1): "turn1_prev", (1, 2): "qk0_next", (1, 3): "qk1_next", (1, 5): "heads0", (1, 6): "max2",
    (1, 7): "qk2_next",
    (2, 1): "qk3_next", (2, 2): "v0_next", (2, 3): "heads1", (2, 5): "max3", (2, 6): "v1_next",
    (2, 7): "out0_prev",
    (3, 1): "out1_prev", (3, 3): "heads2", (3, 5): "max0_next", (3, 7): "turn0",
}
ALL_FILLS = list(FILLS.values())
BANKS_BEFORE = {"qk0_next": 0, "qk1_next": 1, "qk2_next": 2, "qk3_next": 3, "v0_next": 4, "v1_next": 5, "max0_next": 7}
FILLS_BEFORE = list(BANKS_BEFORE)
FIRST_FILLS = [f for f in ALL_FILLS if not f.endswith("_prev")]
LAST_FILLS = [f for f in ALL_FILLS if not f.endswith("_next") or f.startswith("xt")]
TAIL_FILLS = ["heads3_prev", "turn1_prev", "out0_prev", "out1_prev"]
TAIL_AT = {0: "heads3_prev", 2: "turn1_prev", 4: "out0_prev", 5: "out1_prev"}


WEIGHT_SCORES, WEIGHT_VALUES = 2, 4.4
LN_SHARE = 0.8
WEIGHTS = {"heads": 2, "max": 2, "turn": 2, "xt": 2, "qk": 6, "v": 6, "out": 6}
MAX_TILES = 2 * NQ * STEPS
MAX_LEAD = 28


def pieces(n, s):
    if s % 2 == 0:
        return ("scores", "half0", "half1")
    if (n, s - 1) in FILLS:
        return ("scores", "values", "half0", "half1")
    return ("scores", "half0", "half1", "values")


def spread_tiles():
    def weight(n, s, piece):
        share = LN_SHARE if n == 0 and s < 5 else 1
        if piece.startswith("half"):
            return WEIGHTS[FILLS[n, s].split("_")[0][:-1]] / 2 * share if (n, s) in FILLS else 0
        return (WEIGHT_SCORES if piece == "scores" else WEIGHT_VALUES) * share

    steps = [(n, s) for n in range(NQ) for s in range(STEPS)]
    whole = sum(weight(n, s, piece) for n, s in steps for piece in pieces(n, s))
    done, made, out = 0.0, 0, {}
    for n, s in steps:
        out[n, s] = []
        for piece in pieces(n, s):
            done += weight(n, s, piece)
            until = int(MAX_TILES * done / whole + 1e-6)
            out[n, s].append(until - made)
            made = until
    assert made == MAX_TILES
    return out


TILES_AT = spread_tiles()


SPLIT_POOL, SPLIT_DVE, HEADS, OUT = ("qk", "turn"), ("xt",), ("heads",), ("out",)
SPLIT = SPLIT_POOL + SPLIT_DVE
STAGED = SPLIT + HEADS + OUT


def count_before(b, name, kinds):
    def of(fills):
        return len([f for f in fills if f.startswith(kinds)])

    def at(fills):
        return of(fills[:fills.index(name)])

    if isinstance(b, int):
        if b < 0:
            return at(FILLS_BEFORE)
        if b == 0:
            return of(FILLS_BEFORE) + at(FIRST_FILLS)
        if b >= B - 1:
            until = of(FILLS_BEFORE) + of(FIRST_FILLS) + (B - 2) * of(ALL_FILLS)
            return until + (at(LAST_FILLS) if b == B - 1 else of(LAST_FILLS) + at(TAIL_FILLS))
    return b * of(ALL_FILLS) + (of(FILLS_BEFORE) + of(FIRST_FILLS) - of(ALL_FILLS) + at(ALL_FILLS))


def fill_no(b, name):
    return count_before(b, name, ("",))


def slot_of(b, name):
    assert len([f for f in ALL_FILLS if f.startswith(STAGED)]) % 2 == 0
    return count_before(b if isinstance(b, int) else 1, name, STAGED) % 2


def two_before(b, name):
    def of(fills):
        return [f for f in fills if f.startswith(STAGED)]

    if isinstance(b, int) and b < 0:
        fills, earlier = of(FILLS_BEFORE), []
    elif isinstance(b, int) and b == 0:
        fills, earlier = of(FIRST_FILLS), of(FILLS_BEFORE)
    elif isinstance(b, int) and b == B - 1:
        fills, earlier = of(LAST_FILLS), of(ALL_FILLS)
    elif isinstance(b, int) and b >= B:
        fills, earlier = TAIL_FILLS, of(LAST_FILLS)
    else:
        fills, earlier = of(ALL_FILLS), of(ALL_FILLS)
        assert of(FIRST_FILLS)[-2:] == earlier[-2:]
    i = fills.index(name)
    if i >= 2:
        return b, fills[i - 2]
    return (b - 1, earlier[i - 2]) if earlier else None


def build_program(nc, d_x, d_wgu, d_wdn, d_watt, d_bo, d_qb, d_kb, d_diag, d_eye, d_out):
    d_parts = nc.dram_tensor("parts_scratch", (NQ, 2, QH * D, 4, L), F32).ap()
    with ExitStack() as ctx:
        def sem(name):
            return ctx.enter_context(nc.semaphore(name))

        cursor = [-(-nc.sbuf_base // 32) * 32]

        def sb(name, shape, dt=F32, at=None):
            size = 4 * int(np.prod(shape[1:]))
            offset = cursor[0] if at is None else at
            if at is None:
                cursor[0] += -(-size // 32) * 32
            assert offset + size <= nc.sbuf_usable_end
            return nc.alloc_sbuf_tensor_at(name, shape, dt, offset=offset)

        def here():
            return cursor[0]

        x_sb = sb("x_sb", [P, B * TT * C])
        wgu_r = sb("wgu_r", [P, KC, 2 * FF], F32R, at=here())
        wgu = sb("wgu", [P, KC, 2 * FF])
        wdn_r = sb("wdn_r", [P, FT, C], F32R, at=here())
        wdn = sb("wdn", [P, FT, C])
        wqkv = sb("wqkv", [P, 2, KC, 3 * C], F32R)
        wo = sb("wo", [P, 2, KC, C], F32R)
        bo = sb("bo", [P, C])
        eye = sb("eye", [P, P])
        diag = sb("diag", [P, H, P])
        q_aug = sb("q_aug", [P, H, L], F32R)
        wgu_i = sb("wgu_i", [P, KC, 2 * FF], I32, at=here())
        wdn_i = sb("wdn_i", [P, FT, C], I32, at=here() + 4 * KC * 2 * FF)
        k_aug = sb("k_aug", [P, H, L], F32R)
        v_aug = sb("v_aug", [P, TT, H, 2 * D])
        xn = sb("xn", [P, TT, C])
        xnt = sb("xnt", [P, 2, KC, L], F32R)
        row_max = sb("row_max", [P, 2, TT, QH])
        max_in = sb("max_in", [P, TT, 2 * QH])
        den = sb("den", [P, 2, TT, QH, 1])
        stats = sb("stats", [P, 2, TT, 6])
        mean_var = sb("mean_var", [P, 2, TT, 2])
        var = sb("var", [P, 2, TT])
        rstd = sb("rstd", [P, 2, TT])
        newton = sb("newton", [P, 2, TT])
        kept_mean = sb("kept_mean", [P, B * TT])
        kept_rstd = sb("kept_rstd", [P, B * TT])
        w_max = sb("w_max", [P, KC + 2])
        w_top = sb("w_top", [P, 1])
        beyond = sb("beyond", [P, 1], I32)
        own = here()
        hid = sb("hid", [P, 2, L])
        hid_r = sb("hid_r", [P, 2, FT, L], F32R)
        gated = sb("gated", [P, 2, L])
        ffn_end = here()
        w_att = sb("w_att", [P, KC, 4 * C])
        cursor[0] = own
        probs = sb("probs", [P, 2, QH, L])
        parts1 = sb("parts1", [P, 2, 2, L], F32R)
        v_new = sb("v_new", [P, TT, C])
        max_row = sb("max_row", [2 * QH, L], F32R)
        assert here() <= ffn_end
        cursor[0] = ffn_end
        parts = [sb("parts0", [P, 2, 2, L], F32R), parts1]
        heads_t = sb("heads_t", [P, L])
        heads = sb("heads", [P, TT, C])
        att_t = sb("att_t", [P, 2, KC, L], F32R)
        stage = sb("stage", [P, 2, L])

        ps = ctx.enter_context(nc.psum_tensor("ps", [P, 8, L], F32))
        scores_at, max_at, pv, misc = 0, 4, ps[:, 6, :], 7
        gate_at, up_at, turn_at, y_at = 0, 2, 4, 6

        def first(b):
            return isinstance(b, int) and b == 0

        def max_bank(b, tile):
            if first(b) and tile < 2 * STEPS:
                return ps[:, (4, 5, 2, 3)[tile % 4], :], 4
            return ps[:, max_at + tile % 2, :], 2

        def bank_of(b, name):
            return ps[:, BANKS_BEFORE[name] if isinstance(b, int) and b < 0 else misc, :]

        x_in = [sem(f"x_loaded{b}") for b in range(B)]
        gu_in = [sem(f"gu_in{k}") for k in range(KC)]
        dn_in, eye_in, watt_in, att_in, aug_in, stored = (
            sem(n) for n in ("dn_in", "eye_in", "watt_in", "att_in", "aug_in", "stored"))
        w_ready, w_seen, w_reduced, beyond_ready = (sem(n) for n in ("w_ready", "w_seen", "w_reduced", "beyond_ready"))
        watt_hi, watt_ready, w_general = sem("watt_hi"), sem("watt_ready"), sem("w_general")
        ln_step, xn_ready, kept = sem("ln_step"), sem("xn_ready"), sem("kept")
        ffn = [{n: sem(f"{n}_{w}") for n in ("turned", "xnt_ready", "gate_done", "up_done", "gated_ready",
                                             "hid_ready", "hid_hi", "hid_lo", "xnt_hi", "y_done", "y_used")} for w in ("a", "c")]
        ones_set, bo_added = sem("ones_set"), sem("bo_added")
        filled, drained = sem("filled"), sem("drained")
        split_hi = sem("split_hi")
        done = {kinds: sem(f"{kinds[0]}_done") for kinds in (SPLIT_POOL, SPLIT_DVE, HEADS, OUT)}

        def wait_done(eng, b, name):
            kinds = next(k for k in done if name.startswith(k))
            eng.wait_ge(done[kinds], count_before(b, name, kinds) + 1)

        s1_done, s1_used = sem("s1_done"), sem("s1_used")
        neg_hi, neg_ready = sem("neg_hi"), sem("neg_ready")
        aug_done = [sem(f"aug_done{n}") for n in range(NQ)]
        parts_out = sem("parts_out")
        max_moved = sem("max_moved")
        st_done, exp_done, fixed = sem("st_done"), sem("exp_done"), sem("fixed")
        pv_done, heads_t_ready, den_ready, v_ready = (sem(n) for n in ("pv_done", "heads_t_ready", "den_ready", "v_ready"))
        block = ctx.enter_context(nc.Block())

        def wait(eng, s, value):
            if not (isinstance(value, int) and value <= 0):
                eng.wait_ge(s, value)

        def turns(eng, body):
            body(0)
            with eng.Fori(1, B - 1) as b:
                body(b)
            body(B - 1)

        def last(b):
            return isinstance(b, int) and b == B - 1

        def fills_of(b):
            return FIRST_FILLS if first(b) else LAST_FILLS if last(b) else ALL_FILLS

        def x_of(b, tile, n=1):
            at = b * (TT * C) + tile * C
            return x_sb[:, bass.ds(at, n * C)]

        def fill_parts(b, name):
            base = name.split("_")[0]
            seq = b + 1 if name.endswith("_next") else b - 1 if name.endswith("_prev") else b
            return seq, base[:-1], int(base[-1])

        def hi_and_lo(name):
            base = name.split("_")[0]
            kind, part = base[:-1], int(base[-1])
            if kind == "qk":
                return parts[part // 2][:, part % 2, 0, :], parts[part // 2][:, part % 2, 1, :]
            to = xnt if kind == "xt" else att_t
            return to[:, 0, part, :], to[:, 1, part, :]

        @block.sync
        def _(sp):
            sp.dma_start(x_sb[:, 0:TT * C], d_x[0]).then_inc(x_in[0], 16)
            for k in range(KC):
                sp.dma_start(wgu_i[:, k, :], d_wgu[k * P:(k + 1) * P, :]).then_inc(gu_in[k], 16)
            sp.dma_start(eye[:], d_eye).then_inc(eye_in, 16)
            sp.dma_start(wdn_i[:], d_wdn.rearrange("(k p) n -> p k n", p=P)).then_inc(dn_in, 16)
            for b in range(1, B):
                sp.dma_start(x_sb[:, b * TT * C:(b + 1) * TT * C], d_x[b]).then_inc(x_in[b], 16)
                if b == 1:
                    sp.dma_start(w_att[:], d_watt.rearrange("(k p) n -> p k n", p=P)).then_inc(watt_in, 16)
            sp.dma_start(bo[:], d_bo.to_broadcast([P, C])).then_inc(att_in, 16)
            sp.dma_start(diag[:], d_diag).then_inc(att_in, 16)

            def put_parts(quad, of=(0, 1)):
                these = slice((quad % 2) * QH * D, (quad % 2 + 1) * QH * D)
                for is_k in of:
                    for twice in range(2):
                        rows = slice(twice, 4, 2) if is_k else slice(2 * twice, 2 * twice + 2)
                        sp.dma_start(d_parts[quad, is_k, :, rows, :], parts[quad // 2][these, is_k, :, :].bitcast(F32)
                                     ).then_inc(parts_out, 16)

            def get_rows(quad, count):
                sp.wait_ge(parts_out, PUTS * count)
                for is_k, aug in ((0, q_aug), (1, k_aug)):
                    sp.dma_start(aug[0:ROW_BIAS, quad * QH:(quad + 1) * QH, :].bitcast(F32),
                                 d_parts[quad, is_k].rearrange("(h d) r t -> (d r) h t", h=QH)
                                 ).then_inc(aug_done[quad], 16)

            for quad in range(NQ):
                for is_k in range(2):
                    wait_done(sp, -1, f"qk{2 * (quad // 2) + is_k}_next")
                    put_parts(quad, (is_k,))
                get_rows(quad, quad + 1)

            def turn(b):
                for n in range(NQ):
                    if not last(b):
                        if n == 0:
                            wait_done(sp, b, "qk1_next")
                            put_parts(0)
                        elif n == 1:
                            put_parts(1)
                        elif n == 2:
                            wait_done(sp, b, "qk3_next")
                            put_parts(2)
                            put_parts(3)
                        sp.wait_ge(st_done, b * (NQ * STEPS) + (n + 1) * STEPS)
                        get_rows(n, NQ * (b + 1) + (n + 1 if n < 2 else NQ))

            turns(sp, turn)

            def store(b):
                sp.wait_ge(ffn[1]["y_used"], 2 * b + 2)
                sp.dma_start(d_out[b], x_of(b, 0, TT)).then_inc(stored, 16)
            for b in range(B):
                store(b)
            sp.wait_ge(stored, 16 * B)

        @block.gpsimd
        def _(pool):
            pool.wait_ge(w_seen, KC + 2)
            nc.gpsimd.partition_all_reduce(w_top[:, :], w_max[:, KC + 1:KC + 2], P, bass.bass_isa.ReduceOp.max).then_inc(w_reduced, 1)
            def lay_rows():
                pool.wait_ge(w_ready, KC + 1)
                pool.wait_ge(watt_ready, 1)
                for h in range(0, H, H // 2):
                    pool.dma_start(q_aug[ROW_BIAS:ROW_MAX, h:h + H // 2, :], d_qb[:, h:h + H // 2, :]).then_inc(aug_in, 16)
                    pool.dma_start(k_aug[ROW_BIAS:ROWS, h:h + H // 2, :],
                                   d_kb.rearrange("r (o t) -> r o t", o=1).to_broadcast([ROWS - ROW_BIAS, H // 2, L])
                                   ).then_inc(aug_in, 16)
                nc.gpsimd.memset(v_aug[:], 1.0).then_inc(ones_set, 1)
                pool.wait_ge(ones_set, 1)

            def split_hidden(w, b):
                s = ffn[w]
                for f in range(FT):
                    if w == 1 and first(b) and f - 1 in TAIL_AT:
                        take(B, TAIL_AT[f - 1])
                    pool.wait_ge(s["hid_hi"], FT * b + f + 1)
                    nc.gpsimd.tensor_tensor(hid_r[:, 1, f, :], hid[:, f % 2, :], hid_r[:, 0, f, :].bitcast(F32),
                                            ALU.subtract).then_inc(s["hid_lo"], 1)
                if w == 1 and first(b):
                    take(B, TAIL_AT[FT - 1])
                if w == 0 and first(b):
                    lay_rows()

            turns(pool, lambda b: split_hidden(0, b))

            def place_v(b, quad):
                nc.gpsimd.tensor_copy(
                    v_aug[:, :, quad * QH:(quad + 1) * QH, 0:D],
                    v_new[:, :, quad * QH * D:(quad + 1) * QH * D].rearrange("p t (g d) -> p t g d", g=QH),
                ).then_inc(v_ready, 1)

            def split(b, name):
                hi, lo = hi_and_lo(name)
                pool.wait_ge(split_hi, count_before(b, name, SPLIT) + 1)
                nc.gpsimd.tensor_tensor(lo, stage[:, slot_of(b, name), :], hi.bitcast(F32), ALU.subtract
                                        ).then_inc(done[SPLIT_POOL], 1)

            def add_out(b, name):
                seq, kind, part = fill_parts(b, name)
                pool.wait_ge(bo_added, TT * (seq + 1))
                pool.wait_ge(drained, fill_no(b, name) + 1)
                xs = x_of(seq, 2 * part, 2)
                nc.gpsimd.tensor_tensor(xs, stage[:, slot_of(b, name), :], xs, ALU.add).then_inc(done[OUT], 1)

            def take(b, name):
                if name.startswith(SPLIT_POOL):
                    split(b, name)
                elif name.startswith("out"):
                    add_out(b, name)

            for name in FILLS_BEFORE:
                take(-1, name)
            pool.wait_ge(drained, fill_no(-1, "v1_next") + 1)
            for quad in range(3):
                place_v(0, quad)
            pool.wait_ge(att_in, 16 * 2)

            def add_bo(b):
                pool.wait_ge(xn_ready, TT * (B + b) + TT)
                for tile in range(TT):
                    nc.gpsimd.tensor_tensor(x_of(b, tile), x_of(b, tile), bo[:], ALU.add).then_inc(bo_added, 1)

            add_bo(0)

            def turn(b):
                for n in range(NQ):
                    for s in range(STEPS):
                        kt, pair = s // 2, s % 2
                        g = b * (NQ * STEPS) + n * STEPS + s
                        if (n, s) == (0, 3) and not first(b):
                            pool.wait_ge(pv_done, b * (NQ * TT))
                        if (n, s) == (3, 0) and not last(b):
                            pool.wait_ge(pv_done, b * (NQ * TT) + 2 * TT)
                            pool.wait_ge(drained, fill_no(b, "v1_next") + 1)
                        if (n, s) == (3, 4) and not last(b):
                            pool.wait_ge(pv_done, b * (NQ * TT) + 3 * TT)
                        pool.wait_ge(exp_done, g + 1)
                        tile = probs[:, kt % 2, 2 * pair:2 * pair + 2, kt * P:(kt + 1) * P]
                        nc.gpsimd.tensor_tensor(tile, tile, diag[:, n * QH + 2 * pair:n * QH + 2 * pair + 2, :],
                                                ALU.mult).then_inc(fixed, 1)
                        if (n, s) == (0, 3):
                            place_v(b, 3)
                        if not last(b):
                            if (n, s) == (1, 0):
                                add_bo(b + 1)
                            if (n, s) == (3, 0):
                                place_v(b + 1, 0)
                                place_v(b + 1, 1)
                            if (n, s) == (3, 4):
                                place_v(b + 1, 2)
                        name = FILLS.get((n, s))
                        if name in fills_of(b):
                            take(b, name)

            turns(pool, turn)
            turns(pool, lambda b: split_hidden(1, b))

        @block.scalar
        def _(act):
            def ffn_turn(w, b):
                s = ffn[w]

                def hidden_hi(f):
                    act.wait_ge(s["hid_ready"], FT * b + f + 1)
                    if f == 0:
                        wait(act, s["y_done"], 2 * b)
                    nc.scalar.copy(hid_r[:, 0, f, :], hid[:, f % 2, :]).then_inc(s["hid_hi"], 1)

                for f in range(FT):
                    act.wait_ge(s["gate_done"], FT * b + f + 1)
                    wait(act, s["hid_ready"], FT * b + f - 1)
                    nc.scalar.activation(gated[:, f % 2, :], ps[:, gate_at + f % 2, :], ACT.Silu, scale=DEQ
                                         ).then_inc(s["gated_ready"], 1)
                    if f >= 1:
                        hidden_hi(f - 1)
                    if w == 1 and first(b) and f - 1 in TAIL_AT:
                        drain(B, TAIL_AT[f - 1])
                hidden_hi(FT - 1)
                if w == 1 and first(b):
                    drain(B, TAIL_AT[FT - 1])
                if not (w == 1 and last(b)):
                    turned(w, b + 1)

            def turned(w, b):
                s = ffn[w]
                for k in range(KC):
                    if w == 0 and isinstance(b, int) and b == B:
                        act.wait_ge(s["up_done"], FT * B)
                    act.wait_ge(s["turned"], 2 * b + k + 1 - 2 * w)
                    nc.scalar.copy(xnt[:, 0, k, :], ps[:, turn_at + k, :]).then_inc(s["xnt_hi"], 1)

            for k in range(KC):
                act.wait_ge(gu_in[k], 16)
                nc.scalar.copy(wgu_r[:, k, :], wgu_i[:, k, :]).then_inc(w_ready, 1)
            act.wait_ge(dn_in, 16)
            nc.scalar.copy(wdn_r[:], wdn_i[:]).then_inc(w_ready, 1)
            turned(0, 0)
            act.wait_ge(watt_in, 16)
            nc.scalar.copy(wqkv[:, 0, :, :], w_att[:, :, 0:3 * C]).then_inc(watt_hi, 1)
            nc.scalar.copy(wo[:, 0, :, :], w_att[:, :, 3 * C:4 * C]).then_inc(watt_hi, 1)
            turns(act, lambda b: ffn_turn(0, b))

            def drain(b, name):
                at = fill_no(b, name)
                seq, kind, part = fill_parts(b, name)
                bank = bank_of(b, name)
                act.wait_ge(filled, at + 1)
                if kind in STAGED:
                    before = two_before(b, name)
                    if before:
                        wait_done(act, *before)
                    nc.scalar.activation(stage[:, slot_of(b, name), :], bank, ACT.Copy,
                                         scale=D ** -0.5 if kind == "qk" and part % 2 == 0 else 1.0
                                         ).then_inc(drained, 1)
                    if kind in SPLIT:
                        if kind == "qk" and not (isinstance(seq, int) and seq == 0):
                            act.wait_ge(parts_out, (NQ * PUTS) * seq)
                        act.wait_ge(drained, at + 1)
                        nc.scalar.copy(hi_and_lo(name)[0], stage[:, slot_of(b, name), :]).then_inc(split_hi, 1)
                elif kind == "v":
                    if not (isinstance(seq, int) and seq == 0):
                        act.wait_ge(v_ready, NQ * seq)
                    nc.scalar.copy(v_new[:, 2 * part:2 * part + 2, :],
                                   bank.rearrange("p (t c) -> p t c", t=2)).then_inc(drained, 1)
                elif kind == "max":
                    quad_no = seq * NQ + part
                    wait(act, max_moved, quad_no * (16 * 2))
                    nc.scalar.copy(max_row[:, :], bank[0:2 * QH, :]).then_inc(drained, 1)
                    act.wait_ge(drained, at + 1)
                    for i in range(2):
                        act.dma_start(q_aug[ROW_MAX + i:ROW_MAX + i + 1, part * QH:(part + 1) * QH, :].bitcast(F32),
                                      max_row[i * QH:(i + 1) * QH, :].bitcast(F32)).then_inc(max_moved, 16)

            for name in FILLS_BEFORE:
                drain(-1, name)

            def take_heads(quad_no):
                act.wait_ge(pv_done, (quad_no + 1) * TT)
                nc.scalar.copy(heads_t[:, :], pv).then_inc(heads_t_ready, 1)

            def turn(b):
                for n in range(NQ):
                    for s in range(STEPS):
                        kt, pair = s // 2, s % 2
                        quad_no = b * NQ + n
                        g = quad_no * STEPS + s
                        if s == 2 and not (first(b) and n == 0):
                            take_heads(quad_no - 1)
                        act.wait_ge(st_done, g + 1)
                        wait(act, pv_done, quad_no * TT + kt - 1)
                        at = scores_at + 2 * pair
                        nc.scalar.activation(probs[:, kt % 2, 2 * pair:2 * pair + 2, :], ps[:, at:at + 2, :],
                                             ACT.Exp).then_inc(exp_done, 1)
                        name = FILLS.get((n, s))
                        if name in fills_of(b):
                            drain(b, name)

            turns(act, turn)
            take_heads(B * NQ - 1)
            turns(act, lambda b: ffn_turn(1, b))

        @block.vector
        def _(dve):
            def ln_stats(slot, b, tile):
                nc.vector.bn_stats(stats[:, slot, tile, :], x_of(b, tile)).then_inc(ln_step, 1)

            def stats_ready(count):
                dve.wait_ge(ln_step, count)

            def ln_gather(slots):
                for slot in slots:
                    for tile in range(TT):
                        nc.vector.bn_aggr(mean_var[:, slot, tile, :], stats[:, slot, tile, :]).then_inc(ln_step, 1)

            def ln_links(at, slots, which):
                these = slice(slots[0], slots[-1] + 1)
                v, y, t = var[:, these, :], rstd[:, these, :], newton[:, these, :]
                for link in which:
                    dve.wait_ge(ln_step, at + link)
                    if link == 0:
                        ins = nc.vector.tensor_scalar(v, mean_var[:, these, :, 1], EPS, None, ALU.add)
                    elif link == 1:
                        ins = nc.vector.tensor_scalar(y.bitcast(I32), v.bitcast(I32), 1, None, ALU.logical_shift_right)
                    elif link == 2:
                        ins = nc.vector.tensor_scalar(y.bitcast(I32), y.bitcast(I32), -1.0, MAGIC, ALU.mult, ALU.add)
                    elif link % 3 == 0:
                        ins = nc.vector.scalar_tensor_tensor(t, y, -0.5, y, ALU.mult, ALU.mult)
                    elif link % 3 == 1:
                        ins = nc.vector.tensor_tensor(t, t, v, ALU.mult)
                    else:
                        ins = nc.vector.scalar_tensor_tensor(y, t, 1.5, y, ALU.add, ALU.mult)
                    ins.then_inc(ln_step, 1)

            def ln_apply(at, b, tiles):
                for tile in tiles:
                    dve.wait_ge(ln_step, at + LINKS)
                    nc.vector.tensor_scalar(xn[:, tile, :], x_of(b, tile), mean_var[:, 0, tile, 0:1],
                                            rstd[:, 0, tile:tile + 1], ALU.subtract, ALU.mult).then_inc(xn_ready, 1)

            def keep(at, b):
                for to, of in ((kept_mean, mean_var[:, 1, :, 0]), (kept_rstd, rstd[:, 1, :])):
                    dve.wait_ge(ln_step, at + LINKS)
                    nc.vector.tensor_scalar(to[:, bass.ds(b * TT, TT)], of, 1.0, None, ALU.mult).then_inc(kept, 1)

            def apply_kept(b, tiles):
                for tile in tiles:
                    dve.wait_ge(kept, 2 * (b + 1))
                    at = b * TT + tile
                    nc.vector.tensor_scalar(xn[:, tile, :], x_of(b, tile), kept_mean[:, bass.ds(at, 1)],
                                            kept_rstd[:, bass.ds(at, 1)], ALU.subtract, ALU.mult).then_inc(xn_ready, 1)

            def turned(w, b):
                s = ffn[w]
                for k in range(KC):
                    dve.wait_ge(s["xnt_hi"], 2 * b + k + 1 - 2 * w)
                    nc.vector.tensor_tensor(xnt[:, 1, k, :], ps[:, turn_at + k, :], xnt[:, 0, k, :].bitcast(F32),
                                            ALU.subtract).then_inc(s["xnt_ready"], 1)

            one, both = LN_OPS, LN_OPS + 2 * TT
            a_done = one + both * B - TT - 2 * TT
            att_done = a_done + (TT + LINKS) + one

            def ffn_turn(w, b):
                s = ffn[w]
                slots = ((0,) if w == 1 or first(b) else (0, 1) if not last(b) else (1,) if w == 0 else ())
                if w == 1:
                    start = att_done + one * b
                else:
                    start = one if first(b) else one + both * b - TT - TT // 2
                then = not last(b)
                ready = start + (TT if then else 0) + (TT // 2 if 1 in slots else 0)
                at = ready + TT * len(slots)
                for f in range(FT):
                    dve.wait_ge(s["gated_ready"], FT * b + f + 1)
                    dve.wait_ge(s["up_done"], FT * b + f + 1)
                    wait(dve, s["hid_lo"], FT * b + f - 1)
                    if f == 0 and 1 in slots:
                        wait(dve, s["y_used"], 2 * b)
                    if slots and f == 2:
                        stats_ready(ready)
                    if (then or w == 0) and f == (4 if then else 0):
                        wait(dve, s["turned"], 2 * b + 2 - 2 * w)
                    nc.vector.scalar_tensor_tensor(hid[:, f % 2, :], ps[:, up_at + f % 2, :], DEQ, gated[:, f % 2, :],
                                                   ALU.mult, ALU.mult).then_inc(s["hid_ready"], 1)
                    if f == 0 and 1 in slots:
                        ln_stats(1, b - 1, 2)
                        ln_stats(1, b - 1, 3)
                    if then and f < 2:
                        ln_stats(0, b + 1, 2 * f)
                        ln_stats(0, b + 1, 2 * f + 1)
                    if slots and f == 2:
                        ln_gather(slots)
                    if slots and f in (2, 3, 4):
                        ln_links(at, slots, (range(4), range(4, 9), range(9, LINKS))[f - 2])
                    if then and f in (4, 5):
                        ln_apply(at, b + 1, (2 * f - 8, 2 * f - 7))
                    if 1 in slots and f == 5:
                        keep(at, b - 1)
                    if w == 0 and last(b) and f < 2:
                        apply_kept(0, (2 * f, 2 * f + 1))
                    if w == 1 and first(b) and f == 1:
                        divide(B, TAIL_AT[0])
                if not (w == 1 and last(b)):
                    turned(w, b + 1)
                if w == 1 and first(b):
                    wait_done(dve, B, TAIL_FILLS[-1])
                for j in range(2):
                    dve.wait_ge(s["y_done"], 2 * b + j + 1)
                    if w == 0 and j == 1:
                        dve.wait_ge(s["y_used"], 2 * b + 1)
                    nc.vector.scalar_tensor_tensor(x_of(b, 2 * j, 2), ps[:, y_at + j, :], 0.5 * DEQ, x_of(b, 2 * j, 2),
                                                   ALU.mult, ALU.add).then_inc(s["y_used"], 1)
                if w == 0:
                    ln_stats(1, b, 0)
                    ln_stats(1, b, 1)
                if w == 0 and first(b):
                    split_weights()
                    for later in range(2, B):
                        dve.wait_ge(x_in[later], 16)

            def split_weights():
                dve.wait_ge(watt_hi, 2)
                nc.vector.tensor_tensor(wqkv[:, 1, :, :], w_att[:, :, 0:3 * C], wqkv[:, 0, :, :].bitcast(F32),
                                        ALU.subtract).then_inc(watt_ready, 1)
                nc.vector.tensor_tensor(wo[:, 1, :, :], w_att[:, :, 3 * C:4 * C], wo[:, 0, :, :].bitcast(F32),
                                        ALU.subtract).then_inc(watt_ready, 1)

            dve.wait_ge(x_in[0], 16)
            for tile in range(TT):
                ln_stats(0, 0, tile)
            stats_ready(TT)
            ln_gather((0,))
            ln_links(2 * TT, (0,), range(LINKS // 2))

            def largest(column, weights):
                nc.vector.tensor_reduce(w_max[:, column:column + 1], weights, mybir.AxisListType.X, ALU.max,
                                        apply_absolute_value=True).then_inc(w_seen, 1)

            dve.wait_ge(gu_in[0], 16)
            largest(0, wgu_i[:, 0, :])
            ln_links(2 * TT, (0,), range(LINKS // 2, LINKS))
            ln_apply(2 * TT, 0, range(TT))
            for k in range(1, KC):
                dve.wait_ge(gu_in[k], 16)
                largest(k, wgu_i[:, k, :])
            dve.wait_ge(dn_in, 16)
            largest(KC, wdn_i[:].rearrange("p k n -> p (k n)"))
            dve.wait_ge(w_seen, KC + 1)
            largest(KC + 1, w_max[:, 0:KC + 1])
            turned(0, 0)
            dve.wait_ge(w_reduced, 1)
            nc.vector.tensor_scalar(beyond[:, :], w_top[:, :], EXACT, None, ALU.is_gt).then_inc(beyond_ready, 1)
            dve.wait_ge(beyond_ready, 1)
            with dve.If(dve.value_load(beyond[0:1, 0:1], min_val=0, max_val=1) != 0):
                dve.wait_ge(w_ready, KC + 1)
                nc.vector.tensor_copy(wgu[:], wgu_i[:]).then_inc(w_general, 1)
                nc.vector.tensor_copy(wdn[:], wdn_i[:]).then_inc(w_general, 1)
            dve.wait_ge(x_in[1], 16)
            turns(dve, lambda b: ffn_turn(0, b))
            dve.wait_ge(ffn[0]["y_used"], 2 * B)
            ln_stats(1, B - 1, 2)
            ln_stats(1, B - 1, 3)
            stats_ready(a_done)
            ln_gather((1,))
            ln_links(a_done + TT, (1,), range(LINKS))
            keep(a_done + TT, B - 1)

            def row_maxima(b, start, stop):
                for k in range(start, stop):
                    tile = k + MAX_LEAD
                    if last(b) and tile >= MAX_TILES:
                        return
                    quad, u = tile // (2 * STEPS), tile % (2 * STEPS)
                    dve.wait_ge(s1_done, b * MAX_TILES + tile + 1)
                    nc.vector.reduce_max(row_max[:, quad % 2, u % TT, u // TT:u // TT + 1],
                                         max_bank(b, tile)[0], mybir.AxisListType.X).then_inc(s1_used, 1)
                    if u == 2 * STEPS - 1:
                        negate(b * NQ + quad, quad % 2)

            def negate(quad_no, slot):
                dve.wait_ge(s1_used, (quad_no + 1) * (2 * STEPS))
                m = row_max[:, slot, :, :]
                nc.vector.tensor_scalar(max_in[:, :, 0:QH].bitcast(F32R), m, -1.0, None, ALU.mult).then_inc(neg_hi, 1)
                dve.wait_ge(neg_hi, quad_no + 1)
                nc.vector.scalar_tensor_tensor(max_in[:, :, QH:2 * QH], m, -1.0, max_in[:, :, 0:QH],
                                               ALU.mult, ALU.subtract).then_inc(neg_ready, 1)

            def split(b, name):
                hi, lo = hi_and_lo(name)
                dve.wait_ge(split_hi, count_before(b, name, SPLIT) + 1)
                nc.vector.tensor_tensor(lo, stage[:, slot_of(b, name), :], hi.bitcast(F32), ALU.subtract
                                        ).then_inc(done[SPLIT_DVE], 1)

            def divide(b, name):
                seq, kind, part = fill_parts(b, name)
                got = stage[:, slot_of(b, name), :].rearrange("p (t g d) -> p t g d", t=TT, g=QH)
                dve.wait_ge(drained, fill_no(b, name) + 1)
                nc.vector.reciprocal(den[:, part % 2, :, :, :], got[:, :, :, D:D + 1]).then_inc(den_ready, 1)
                dve.wait_ge(den_ready, seq * NQ + part + 1)
                nc.vector.tensor_tensor(
                    heads[:, :, part * QH * D:(part + 1) * QH * D].rearrange("p t (g d) -> p t g d", g=QH),
                    got[:, :, :, 0:D], den[:, part % 2, :, :, :].to_broadcast([P, TT, QH, D]), ALU.mult
                ).then_inc(done[HEADS], 1)

            row_maxima(0, -MAX_LEAD, 0)

            def turn(b):
                at = att_done - LINKS
                made = 0
                for n in range(NQ):
                    for s in range(STEPS):
                        count = sum(TILES_AT[n, s])
                        starting = last(b) and n == 0
                        if starting and s == 0:
                            wait_done(dve, 1, "out1_prev")
                            ln_stats(0, 0, 0)
                            ln_stats(0, 0, 1)
                        if starting and s == 1:
                            stats_ready(at - TT)
                        row_maxima(b, made, made + (count + 1) // 2)
                        if starting and s == 0:
                            ln_stats(0, 0, 2)
                            ln_stats(0, 0, 3)
                        elif starting and s == 1:
                            ln_gather((0,))
                        elif starting and 2 <= s < 4:
                            ln_links(at, (0,), range(5 * s - 8, 5 * s - 6))
                        elif starting and s == 5:
                            ln_apply(at, 0, (2,))
                        elif n == 0 and 1 <= s < 3 and not last(b):
                            apply_kept(b + 1, (2 * s - 2,))
                        row_maxima(b, made + (count + 1) // 2, made + count)
                        made += count
                        if starting and s == 1:
                            ln_links(at, (0,), (0, 1))
                        elif starting and 2 <= s < 4:
                            ln_links(at, (0,), range(5 * s - 6, 5 * s - 3))
                        elif starting and s == 4:
                            ln_apply(at, 0, (0, 1))
                        elif starting and s == 5:
                            ln_apply(at, 0, (3,))
                        elif n == 0 and 1 <= s < 3 and not last(b):
                            apply_kept(b + 1, (2 * s - 1,))
                        name = FILLS.get((n, s))
                        if name in fills_of(b) and name.startswith(HEADS):
                            divide(b, name)
                        if name in fills_of(b) and name.startswith(SPLIT_DVE):
                            split(b, name)

            turns(dve, turn)
            turns(dve, lambda b: ffn_turn(1, b))

        @block.tensor
        def _(pe):
            def matmul(out, lhs, rhs, start, stop, **k):
                return nc.tensor.matmul(out, lhs, rhs, start=start, stop=stop, **k)

            def turn_x(w, b):
                s = ffn[w]
                pe.wait_ge(xn_ready, TT * (2 * w * B + b + 1))
                if w == 1:
                    wait(pe, s["xnt_ready"], 2 * b - 2)
                else:
                    wait(pe, s["xnt_ready"], 2 * b)
                for k in range(KC):
                    for t in range(TT):
                        ins = nc.tensor.transpose(ps[:, turn_at + k, t * P:(t + 1) * P],
                                                  xn[:, t, k * P:(k + 1) * P], eye[:])
                    ins.then_inc(s["turned"], 1)

            def split_products(out, lhs, lhs_at, rhs, rhs_at, halves=range(KC)):
                for k in halves:
                    for a, c in ((0, 0), (0, 1), (1, 0)):
                        ins = matmul(out, lhs[:, a, k, lhs_at], rhs[:, c, k, rhs_at], (k, a, c) == (0, 0, 0),
                                     (k, a, c) == (KC - 1, 1, 0))
                return ins

            def fill(b, name, halves=(0, 1)):
                at = fill_no(b, name)
                seq, kind, part = fill_parts(b, name)
                tiles = [t for half in halves for t in (2 * half, 2 * half + 1)]
                bank = bank_of(b, name)
                bank_tiles = bank.rearrange("p (t c) -> p t c", t=2)
                if halves[0] == 0 and not (isinstance(b, int) and b < 0 and name != "max0_next"):
                    wait(pe, drained, at)
                if kind == "xt":
                    if halves[0] == 0:
                        pe.wait_ge(xn_ready, TT * (B + seq + 1))
                    for t in tiles:
                        ins = nc.tensor.transpose(bank[:, t * P:(t + 1) * P], xn[:, t, part * P:(part + 1) * P], eye[:])
                elif kind == "qk":
                    if name == "qk0_next" and not (isinstance(b, int) and b < 0):
                        wait_done(pe, b, "xt1_next")
                    w0 = (part % 2) * C + (part // 2) * P
                    ins = split_products(bank, wqkv, slice(w0, w0 + P), xnt, slice(0, L), halves)
                elif kind == "v":
                    for t in halves:
                        tok = (2 * part + t) * P
                        ins = split_products(bank_tiles[:, t, :], xnt, slice(tok, tok + P), wqkv, slice(2 * C, 3 * C))
                elif kind == "max":
                    if halves[0] == 0:
                        pe.wait_ge(neg_ready, seq * NQ + part + 1)
                    for t in tiles:
                        ins = nc.tensor.transpose(bank[0:2 * QH, t * P:(t + 1) * P], max_in[:, t, :], eye[:])
                elif kind == "heads":
                    if halves[0] == 0:
                        pe.wait_ge(heads_t_ready, seq * NQ + part + 1)
                    for t in tiles:
                        ins = nc.tensor.transpose(bank[:, t * P:(t + 1) * P], heads_t[:, t * P:(t + 1) * P], eye[:])
                elif kind == "turn":
                    if halves[0] == 0:
                        wait_done(pe, b, "heads1" if part == 0 else "heads3_prev")
                    for t in tiles:
                        ins = nc.tensor.transpose(bank[:, t * P:(t + 1) * P], heads[:, t, part * P:(part + 1) * P], eye[:])
                elif kind == "out":
                    if name == "out0_prev":
                        wait_done(pe, b, "turn1_prev")
                    for t in halves:
                        tok = (2 * part + t) * P
                        ins = split_products(bank_tiles[:, t, :], att_t, slice(tok, tok + P), wo, slice(0, C))
                if halves[-1] == 1:
                    ins.then_inc(filled, 1)

            def ffn_turn(w, b):
                s = ffn[w]
                if w == 0:
                    pe.wait_ge(s["xnt_ready"], 2 * b + 2)
                else:
                    wait(pe, s["xnt_ready"], 2 * b)
                either(lambda weights, r: gate_up(weights[0], r, s, b))
                wait(pe, s["y_used"], 2 * b)
                if w == 1 and first(b):
                    pe.wait_ge(drained, fill_no(B, TAIL_FILLS[-1]) + 1)
                either(lambda weights, r: down(weights[1], r, w, b))

            def either(products):
                with pe.If(general != 0):
                    pe.wait_ge(w_general, 2)
                    products((wgu, wdn), F32)
                with pe.Else():
                    products((wgu_r, wdn_r), F32R)

            def gate_up(weights, dtype, s, b):
                for f in range(FT):
                    wait(pe, s["hid_ready"], FT * b + f - 1)
                    for which, at, done in ((0, gate_at, "gate_done"), (1, up_at, "up_done")):
                        w0 = which * FF + f * P
                        for k in range(KC):
                            for part in range(2):
                                moving = xnt[:, part, k, :]
                                ins = matmul(ps[:, at + f % 2, :], weights[:, k, w0:w0 + P],
                                             moving if dtype == F32R else moving.bitcast(F32),
                                             k == 0 and part == 0, k == KC - 1 and part == 1)
                        ins.then_inc(s[done], 1)
                    if s is ffn[1] and first(b) and f in TAIL_AT:
                        fill(B, TAIL_AT[f])
                    if s is ffn[0] and last(b) and f == FT - 2:
                        turn_x(0, b + 1)

            def down(weights, dtype, w, b):
                s = ffn[w]
                for f in range(FT):
                    if f == 3 and not last(b):
                        turn_x(w, b + 1)
                    if f == 2 and last(b) and w == 0:
                        pe.wait_ge(s["xnt_ready"], 2 * (B + 1))
                        pe.wait_ge(s["hid_ready"], FT * B)
                        pe.wait_ge(watt_ready, 2)
                        fill(-1, "qk0_next")
                        fill(-1, "qk1_next")
                    for part in range(2):
                        pe.wait_ge(s["hid_lo" if part else "hid_hi"], FT * b + f + 1)
                        for t in range(TT):
                            out = ps[:, y_at + t // 2, (t % 2) * C:(t % 2 + 1) * C]
                            tokens = hid_r[:, part, f, t * P:(t + 1) * P]
                            ins = matmul(out, tokens if dtype == F32R else tokens.bitcast(F32), weights[:, f, :],
                                         f == 0 and part == 0 and t % 2 == 0, f == FT - 1 and part == 1,
                                         skip_group_check=True)
                            if f == FT - 1 and part == 1 and t % 2 == 1:
                                ins.then_inc(s["y_done"], 1)

            pe.wait_ge(eye_in, 16)
            turn_x(0, 0)
            pe.wait_ge(w_ready, KC + 1)
            pe.wait_ge(beyond_ready, 1)
            general = pe.value_load(beyond[0:1, 0:1], min_val=0, max_val=1)
            turns(pe, lambda b: ffn_turn(0, b))

            def scores_for_max(b, start, stop):
                for k in range(start, stop):
                    tile = k + MAX_LEAD
                    if last(b) and tile >= MAX_TILES:
                        return
                    quad, u = (tile // (2 * STEPS)) % NQ, tile % (2 * STEPS)
                    seq = b + tile // MAX_TILES
                    h, t = quad * QH + u // TT, u % TT
                    if u == 0:
                        pe.wait_ge(aug_done[quad], (seq + 1) * (16 * 2))
                    bank, back = max_bank(b, tile)
                    wait(pe, s1_used, b * MAX_TILES + tile + 1 - back)
                    matmul(bank, q_aug[0:ROW_MAX, h, t * P:(t + 1) * P], k_aug[0:ROW_MAX, h, :],
                           True, True).then_inc(s1_done, 1)

            def weigh_values(quad_no, quad, kt, seq):
                pe.wait_ge(fixed, quad_no * STEPS + 2 * kt + 2)
                if kt == 0:
                    pe.wait_ge(v_ready, seq * NQ + quad + 1)
                    wait(pe, heads_t_ready, quad_no)
                for g in range(QH):
                    ins = matmul(pv[32 * g:32 * g + 32, :], v_aug[:, kt, quad * QH + g, :], probs[:, kt % 2, g, :],
                                 kt == 0, kt == TT - 1, skip_group_check=True)
                ins.then_inc(pv_done, 1)

            for name in FILLS_BEFORE[2:-1]:
                fill(-1, name)
            pe.wait_ge(aug_in, 16 * 4)
            pe.wait_ge(drained, fill_no(-1, FILLS_BEFORE[-1]))
            pe.wait_ge(ffn[0]["y_used"], 2 * B)
            scores_for_max(0, -MAX_LEAD, 2 * STEPS - MAX_LEAD)
            fill(-1, FILLS_BEFORE[-1])
            scores_for_max(0, 2 * STEPS - MAX_LEAD, 0)

            def turn(b):
                made = 0
                for n in range(NQ):
                    for s in range(STEPS):
                        kt, pair = s // 2, s % 2
                        quad_no = b * NQ + n
                        g = quad_no * STEPS + s
                        if s == 0:
                            pe.wait_ge(max_moved, (quad_no + 1) * (16 * 2))
                        wait(pe, exp_done, g - 1)
                        for i in range(2):
                            h = n * QH + 2 * pair + i
                            ins = matmul(ps[:, scores_at + 2 * pair + i, :], k_aug[0:ROWS, h, kt * P:(kt + 1) * P],
                                         q_aug[0:ROWS, h, :], True, True)
                        ins.then_inc(st_done, 1)
                        name = FILLS.get((n, s))
                        for piece, count in zip(pieces(n, s), TILES_AT[n, s]):
                            if piece == "values" and s > 1:
                                weigh_values(quad_no, n, (s - 3) // 2, b)
                            elif piece == "values" and not (first(b) and n == 0):
                                weigh_values(quad_no - 1, (n - 1) % NQ, TT - 1, b)
                            elif piece.startswith("half") and name in fills_of(b):
                                fill(b, name, (int(piece[-1]),))
                            scores_for_max(b, made, made + count)
                            made += count

            turns(pe, turn)
            weigh_values(B * NQ - 1, NQ - 1, TT - 1, B - 1)
            pe.wait_ge(exp_done, B * NQ * STEPS)
            turns(pe, lambda b: ffn_turn(1, b))


def kernel(**inputs):
    import concourse.bacc as bacc
    from concourse.bass_utils import run_bass_kernel_spmd

    def laid(a):
        return np.ascontiguousarray(a)

    x = np.asarray(inputs["L0_attn_q"])
    arrays = {
        "x_in": laid(x.reshape(B, TT, P, C).transpose(0, 2, 1, 3)).reshape(B, P, TT * C),
        "w_gate_up": laid(np.concatenate([np.asarray(inputs["L0_ffn_w_gate"]).T,
                                          np.asarray(inputs["L0_ffn_w_up"]).T], axis=1)),
        "w_down": laid(np.asarray(inputs["L0_ffn_w_down"]).T),
        "w_att": laid(np.concatenate([np.asarray(inputs[f"L0_attn_W{n}"]).T for n in "qkvo"], axis=1)),
        "b_out": laid(np.asarray(inputs["L0_attn_bo"]).reshape(1, C)),
        **tables(),
    }
    nc = bacc.Bacc("TRN2", target_bir_lowering=False, num_devices=1, dynamic_dma_scratch_size=4096)
    args = [nc.dram_tensor(n, a.shape, mybir.dt.from_np(a.dtype), kind="ExternalInput").ap() for n, a in arrays.items()]
    args.append(nc.dram_tensor("x_out", (B, P, TT * C), F32, kind="ExternalOutput").ap())
    build_program(nc, *args)
    out = run_bass_kernel_spmd(nc, [arrays], core_ids=[0]).results[0]["x_out"]
    return laid(out.reshape(B, P, TT, C).transpose(0, 2, 1, 3)).reshape(B, L, C)
```
